# Optimizing a Trainium2 kernel written in Bass

```python
import numpy as np
import jax
import jax.numpy as jnp

def _softmax(x, axis=-1):
    return jax.nn.softmax(x, axis=axis)

def _gelu(x):
    return jax.nn.gelu(x, approximate=True)

def _silu(x):
    return jax.nn.silu(x)

def _sigmoid(x):
    return jax.nn.sigmoid(x)

def _layernorm(x, axis=-1, eps=1e-05):
    m = jnp.mean(x, axis=axis, keepdims=True)
    v = jnp.var(x, axis=axis, keepdims=True)
    return (x - m) / jnp.sqrt(v + eps)

def _scatter_add(tgt, idx, src, axis=0):
    return tgt.at[idx].add(src)

def _segment_sum(src, seg, n):
    return jax.ops.segment_sum(src, seg, n)
kernel_name = 'mk_macaron_d1_jaxref_r8_84b541'

def setup_inputs(seed: int=0):
    np.random.seed(seed)
    _w = jnp.asarray

    def _L0_attn_setup():
        import jax, jax.numpy as jnp
        import numpy as np
        B, T, C = (64, 32, 128)
        N_HEAD, HEAD_SIZE, KV_RANK = (16, 64, 128)
        BLOCK_SIZE = 32
        key = jax.random.key(seed)
        ks = jax.random.split(key, 5)
        HD = N_HEAD * HEAD_SIZE

        def init(k, shape):
            fan_in = shape[0]
            bound = 1.0 / np.sqrt(fan_in)
            return jax.random.uniform(k, shape, jnp.float32, -bound, bound)
        return {'x': jax.random.normal(ks[0], (B, T, C), jnp.float32), 'w_kv_down': init(ks[1], (C, KV_RANK)), 'w_kv_up': init(ks[2], (KV_RANK, 2 * HD)), 'w_q': init(ks[3], (C, HD)), 'w_out': init(ks[4], (HD, C))}
    _L0_attn_in = _L0_attn_setup()

    def _L0_ffn_setup():
        import jax, jax.numpy as jnp
        import numpy as np
        import math
        MAX_NORM = 0.95
        CURVATURE = 1.0
        TOP_K = 2
        EPS = 1e-07

        def _project_to_ball(x):
            norm = jnp.clip(jnp.linalg.norm(x, axis=-1, keepdims=True), EPS, None)
            scale = jnp.where(norm > MAX_NORM, MAX_NORM / norm, jnp.ones_like(norm))
            return x * scale
        key = jax.random.key(seed)
        ks = jax.random.split(key, 8)
        B, N, D, E, F = (2, 256, 128, 8, 512)
        x = jax.random.normal(ks[0], (B, N, D), dtype=jnp.float32)
        c = jax.random.normal(ks[1], (E, D), dtype=jnp.float32)
        centroids = c / jnp.linalg.norm(c, axis=-1, keepdims=True) * 0.5
        Wp = jax.random.normal(ks[2], (D, D), dtype=jnp.float32) * 0.02
        bp = jnp.zeros((D,), dtype=jnp.float32)
        W1 = jax.random.normal(ks[3], (E, D, F), dtype=jnp.float32) * 0.02
        b1 = jnp.zeros((E, F), dtype=jnp.float32)
        W2 = jax.random.normal(ks[4], (E, F, D), dtype=jnp.float32) * 0.02
        b2 = jnp.zeros((E, D), dtype=jnp.float32)
        return {'x': x, 'centroids': centroids, 'Wp': Wp, 'bp': bp, 'W1': W1, 'b1': b1, 'W2': W2, 'b2': b2}
    _L0_ffn_in = _L0_ffn_setup()
    _d = {'L0_attn_x': _L0_attn_in['x'], 'L0_attn_w_kv_down': _L0_attn_in['w_kv_down'], 'L0_attn_w_kv_up': _L0_attn_in['w_kv_up'], 'L0_attn_w_q': _L0_attn_in['w_q'], 'L0_attn_w_out': _L0_attn_in['w_out'], 'L0_ffn_centroids': _L0_ffn_in['centroids'], 'L0_ffn_Wp': _L0_ffn_in['Wp'], 'L0_ffn_bp': _L0_ffn_in['bp'], 'L0_ffn_W1': _L0_ffn_in['W1'], 'L0_ffn_b1': _L0_ffn_in['b1'], 'L0_ffn_W2': _L0_ffn_in['W2'], 'L0_ffn_b2': _L0_ffn_in['b2']}
    _x0 = _d['L0_attn_x']
    _d['L0_attn_x'] = jax.random.normal(jax.random.fold_in(jax.random.key(seed), 1), (16, 256, 128), dtype=_x0.dtype)
    del _x0
    return _d

def reference(L0_attn_x, L0_attn_w_kv_down, L0_attn_w_kv_up, L0_attn_w_q, L0_attn_w_out, L0_ffn_centroids, L0_ffn_Wp, L0_ffn_bp, L0_ffn_W1, L0_ffn_b1, L0_ffn_W2, L0_ffn_b2):

    def _L0_attn_ref(x, w_kv_down, w_kv_up, w_q, w_out):
        import jax, jax.numpy as jnp
        import numpy as np
        B, T, C = (64, 32, 128)
        N_HEAD, HEAD_SIZE, KV_RANK = (16, 64, 128)
        BLOCK_SIZE = 32
        Bx, Tx, Cx = x.shape
        HD = N_HEAD * HEAD_SIZE
        latent_kv = x @ w_kv_down
        kv = latent_kv @ w_kv_up
        k, v = (kv[..., :HD], kv[..., HD:])
        k = k.reshape(Bx, Tx, N_HEAD, HEAD_SIZE)
        v = v.reshape(Bx, Tx, N_HEAD, HEAD_SIZE)
        q = (x @ w_q).reshape(Bx, Tx, N_HEAD, HEAD_SIZE)
        scale = HEAD_SIZE ** (-0.5)
        att = jnp.einsum('bqhd,bkhd->bhqk', q, k) * scale
        causal = jnp.tril(jnp.ones((Tx, Tx), dtype=bool))
        att = jnp.where(causal, att, -jnp.inf)
        att = jax.nn.softmax(att, axis=-1)
        y = jnp.einsum('bhqk,bkhd->bqhd', att, v)
        y = y.reshape(Bx, Tx, HD)
        return y @ w_out

    def _L0_ffn_ref(x, centroids, Wp, bp, W1, b1, W2, b2):
        import jax, jax.numpy as jnp
        import numpy as np
        import math
        MAX_NORM = 0.95
        CURVATURE = 1.0
        TOP_K = 2
        EPS = 1e-07

        def _project_to_ball(x):
            norm = jnp.clip(jnp.linalg.norm(x, axis=-1, keepdims=True), EPS, None)
            scale = jnp.where(norm > MAX_NORM, MAX_NORM / norm, jnp.ones_like(norm))
            return x * scale
        B, N, D = x.shape
        E = centroids.shape[0]
        x_hyper = _project_to_ball(x @ Wp + bp)
        c_proj = _project_to_ball(centroids)
        x_norm_sq = jnp.sum(x_hyper * x_hyper, axis=-1)
        c_norm_sq = jnp.sum(c_proj * c_proj, axis=-1)
        x_norm_sq = jnp.clip(x_norm_sq, None, 0.99)
        c_norm_sq = jnp.clip(c_norm_sq, None, 0.99)
        dot = jnp.einsum('bnd,ed->bne', x_hyper, c_proj)
        diff_sq = jnp.maximum(x_norm_sq[..., None] + c_norm_sq - 2.0 * dot, 0.0)
        denom = (1.0 - x_norm_sq)[..., None] * (1.0 - c_norm_sq) + EPS
        arg = jnp.clip(1.0 + 2.0 * diff_sq / denom, 1.0 + EPS, None)
        dist = jnp.arccosh(arg)
        routing_logits = -dist / math.sqrt(CURVATURE)
        top_v, top_i = jax.lax.top_k(routing_logits, TOP_K)
        top_w = jax.nn.softmax(top_v, axis=-1)
        comb = jnp.sum(jax.nn.one_hot(top_i, E, dtype=x.dtype) * top_w[..., None], axis=2)
        h = jax.nn.gelu(jnp.einsum('bnd,edf->bnef', x, W1) + b1, approximate=False)
        y = jnp.einsum('bnef,efd->bned', h, W2) + b2
        out = jnp.einsum('bne,bned->bnd', comb, y)
        return out
    x = L0_attn_x
    x = x + 0.5 * _L0_ffn_ref(_layernorm(x, axis=-1), L0_ffn_centroids, L0_ffn_Wp, L0_ffn_bp, L0_ffn_W1, L0_ffn_b1, L0_ffn_W2, L0_ffn_b2)
    x = x + _L0_attn_ref(_layernorm(x, axis=-1), L0_attn_w_kv_down, L0_attn_w_kv_up, L0_attn_w_q, L0_attn_w_out)
    x = x + 0.5 * _L0_ffn_ref(_layernorm(x, axis=-1), L0_ffn_centroids, L0_ffn_Wp, L0_ffn_bp, L0_ffn_W1, L0_ffn_b1, L0_ffn_W2, L0_ffn_b2)
    return x

_drawn_inputs = setup_inputs


def setup_inputs(seed=0):
    import zlib

    import numpy as np

    out = dict(_drawn_inputs(seed))
    spreads = {'L0_ffn_bp': (0.0, 0.1), 'L0_ffn_b1': (0.0, 0.44), 'L0_ffn_b2': (0.0, 0.1)}
    factors = {'L0_attn_w_q': 7.938}
    for name, (base, spread) in spreads.items():
        noise = np.random.default_rng([zlib.crc32(name.encode()), seed]).standard_normal(out[name].shape)
        drawn = base * np.exp(spread * noise) if base else spread * noise
        out[name] = jnp.asarray(drawn.astype(out[name].dtype))
    for name, factor in factors.items():
        out[name] = (out[name] * factor).astype(out[name].dtype)
    return out
```

```python
import concourse.bass as bass
from concourse import mybir
from contextlib import ExitStack

F32 = mybir.dt.float32
F32R = mybir.dt.float32r
BF16 = mybir.dt.bfloat16
ALU = mybir.AluOpType
ACT = mybir.ActivationFunctionType
AX = mybir.AxisListType

P = 128
CREDIT = 2


def macaron_block(nc, x, w_down, wq_t, wuk_t, wuv_t, w_out, centroids, wp_t, wp, bp, w1, b1, w2, b2, out):
    BATCH, SEQ, D = x.shape
    HD, HEADS, _ = wq_t.shape
    E, FC = w1.shape[1], w1.shape[2] // P
    TOKENS = BATCH * SEQ
    TILES = TOKENS // P
    QT = SEQ // P
    GROUP = 4
    GROUPS = TILES // GROUP
    WT = 8
    WIDE = WT * P
    PASSES = TOKENS // WIDE
    STEPS = E * FC
    UNITS = BATCH * HEADS
    LN_EPS, BALL_EPS, MAX_NORM, MAX_SQ = 1e-5, 1e-7, 0.95, 0.99
    HALF = GROUP * P
    R_COLS = D + E
    PC = QT * (QT + 1) // 2 * P
    assert QT == 2 and WIDE == 2 * HALF and FC == 4

    ctx = ExitStack()
    with ctx:
        def sb(name, shape, dt=F32):
            return ctx.enter_context(nc.sbuf_tensor(name, shape, dt))

        def sem(name):
            return ctx.enter_context(nc.semaphore(name))

        x_tok = sb("x_tok", [P, TILES, D])
        xn = sb("xn", [P, TILES, D])
        xT = sb("xT", [P, TOKENS])
        xhi = sb("xhi", [P, TOKENS], F32R)
        xlo = sb("xlo", [P, TOKENS], F32R)
        w1_hi = sb("w1_hi", [P, E, FC * P], F32R)
        w1_lo = sb("w1_lo", [P, E, FC * P], F32R)
        w2_hi = sb("w2_hi", [P, E, FC, D], F32R)
        w2_lo = sb("w2_lo", [P, E, FC, D], F32R)
        a_hi = sb("a_hi", [P, HEADS, D], F32R)
        a_lo = sb("a_lo", [P, HEADS, D], F32R)
        b_hi = sb("b_hi", [P, HEADS, D], F32R)
        b_lo = sb("b_lo", [P, HEADS, D], F32R)
        ring_hi = sb("ring_hi", [P, 2, WIDE], F32R)
        ring_lo = sb("ring_lo", [P, 2, WIDE], F32R)
        work = sb("work", [P, 2, WIDE])
        ident = sb("ident", [P, P])
        ident_bf = sb("ident_bf", [P, P], BF16)
        causal_bf = sb("causal_bf", [P, P], BF16)
        ones = sb("ones", [P, 1])
        comb = sb("comb", [P, TILES, E])
        comb_cur = sb("comb_cur", [P, WT, E])
        stats = sb("stats", [P, TILES, 6])
        mean_var = sb("mean_var", [P, TILES, 2])
        std = sb("std", [P, TILES])
        rstd = sb("rstd", [P, TILES])
        router_w = sb("router_w", [P, R_COLS])
        router_b = sb("router_b", [P, R_COLS])
        cent = sb("cent", [E, D])
        cent_s = sb("cent_s", [E, 4])
        cent_t = sb("cent_t", [P, E])
        cent_sq = sb("cent_sq", [P, E])
        cn2 = sb("cn2", [P, 2, E])
        rank = sb("rank", [P, E])
        bp_col = sb("bp_col", [P, 1])
        b1_sb = sb("b1_sb", [P, E, FC])
        b2_sb = sb("b2_sb", [P, E])
        tok_s = sb("tok_s", [P, 8, TILES])

        h_ring = xT[:, 0:2 * WIDE].rearrange("p (r n) -> p r n", r=2)
        y_acc = xT[:, 2 * WIDE:3 * WIDE]
        y_one = xT[:, 3 * WIDE:4 * WIDE]
        comb_b = xn[:, 0:2 * WT, :].rearrange("p (r t) d -> p r (t d)", r=2)
        r_dot = comb
        TE = TILES * E
        r_buf = [xT[:, k * TE:(k + 1) * TE].rearrange("p (t e) -> p t e", e=E) for k in range(8)]
        lat_tok = xn
        lat_T = xT
        stage = [work[:, k, 0:WIDE] for k in range(2)]
        flat = work[:, :, :].rearrange("p a b -> p (a b)")
        q_ring = [flat[:, k * SEQ:(k + 1) * SEQ] for k in range(2)]
        at = 2 * SEQ
        p_ring = [flat[:, at + k * PC:at + (k + 1) * PC] for k in range(2)]
        at += 2 * PC
        pt_ring = [flat[:, at + k * PC:at + (k + 1) * PC] for k in range(2)]
        at += 2 * PC
        o_sb = tok_s[:, :, :].rearrange("p a b -> p (a b)")
        lat_cur = sb("lat_cur", [P, QT, P])
        neg_max = sb("neg_max", [P, 2, QT])
        row_sum = sb("row_sum", [P, 2, QT])
        row_rec = sb("row_rec", [P, 2, QT])
        assert at <= 2 * WIDE

        pair = [ctx.enter_context(nc.psum_tensor(f"pair{k}", [P, 2 * HALF], F32)) for k in range(4)]
        h_ps = pair[0:2]
        y_ps = pair[2]
        c_ps = pair[3]
        bank = [pair[k // 2][:, (k % 2) * HALF:(k % 2 + 1) * HALF] for k in range(8)]
        s_bank, t_bank, z_bank = bank[0:2], bank[2:4], bank[4:6]
        q_bank, o_bank = bank[6], bank[7]

        small_loaded, stored = sem("small_loaded"), sem("stored")
        x_loaded = [sem(f"x_loaded{g}") for g in range(4)]
        staged = [sem(f"staged{k}") for k in range(2)]
        consts_ready = sem("consts_ready")
        xt_ready = sem("xt_ready")
        prep_mm = sem("prep_mm")
        route_mm = sem("route_mm")
        lat_mm = sem("lat_mm")
        l1_done = sem("l1_done")
        l2_done = sem("l2_done")
        combT_done = sem("combT_done")
        accT_done = sem("accT_done")
        q_done = sem("q_done")
        s_done = sem("s_done")
        t_done = sem("t_done")
        z_done = sem("z_done")
        o_done = sem("o_done")
        oT_done = sem("oT_done")
        sqrt_done = sem("sqrt_done")
        xhi_done = sem("xhi_done")
        gelu_done = sem("gelu_done")
        exp_done = sem("exp_done")
        pt_done = sem("pt_done")
        zhi_done = sem("zhi_done")
        wsplit_hi = sem("wsplit_hi")
        dve_chain = sem("dve_chain")
        root_in = sem("root_in")
        norm_done = sem("norm_done")
        xlo_done = sem("xlo_done")
        w_done = sem("w_done")
        r_done = sem("r_done")
        lat_done = sem("lat_done")
        combcur_done = sem("combcur_done")
        comb_ready = sem("comb_ready")
        lo_done = sem("lo_done")
        combs_done = sem("combs_done")
        one_done = sem("one_done")
        acc_done = sem("acc_done")
        xup_done = sem("xup_done")
        qev_done = sem("qev_done")
        max_done = sem("max_done")
        rec_done = sem("rec_done")
        pn_done = sem("pn_done")
        zlo_done = sem("zlo_done")
        latcur_done = sem("latcur_done")
        oev_done = sem("oev_done")
        xres_done = sem("xres_done")

        def did(n):
            return n + CREDIT

        block = ctx.enter_context(nc.Block())

        W_CHUNKS = 2 * (E * FC * P // WIDE)
        HH = HEADS // 2
        HW = HH * D
        AB = 4

        @block.sync
        def _(sp):
            x_t = x.rearrange("b (q p) d -> p (b q) d", p=P)
            for g in range(4):
                n = TILES // 4
                sp.dma_start(x_tok[:, g * n:(g + 1) * n, :], x_t[:, g * n:(g + 1) * n, :]).then_inc(x_loaded[g], 16)
            half = W_CHUNKS // 2
            for k in range(W_CHUNKS):
                if k >= 2:
                    sp.wait_ge(w_done, did(k - 1))
                src = (w1, w2)[k // half].rearrange("p e n -> p (e n)")[:, (k % half) * WIDE:(k % half + 1) * WIDE]
                sp.dma_start(stage[k % 2], src).then_inc(staged[k % 2], 16)
            for k in range(AB):
                sp.wait_ge(w_done, did(W_CHUNKS + k))
                left, right = ((wq_t, wuk_t), (wuv_t, w_out))[k // 2]
                for slot, w in ((0, left), (1, right)):
                    sp.dma_start(stage[slot][0:HD, 0:HW], w.rearrange("p h d -> p (h d)")[:, (k % 2) * HW:(k % 2 + 1) * HW]) \
                        .then_inc(staged[slot], 16)
            out_t = out.rearrange("b (q p) d -> p (b q) d", p=P)
            for t in range(PASSES):
                sp.wait_ge(xup_done, did(PASSES + t + 1))
                sp.dma_start(out_t[:, t * WT:(t + 1) * WT, :], x_tok[:, t * WT:(t + 1) * WT, :]).then_inc(stored, 16)
            sp.wait_ge(stored, 16 * PASSES)

        @block.gpsimd
        def _(pool):
            nc.gpsimd.memset(ident[:], 0.0).then_inc(consts_ready, 1)
            nc.gpsimd.memset(causal_bf[:], 0.0).then_inc(consts_ready, 1)
            nc.gpsimd.memset(ones[:], 1.0).then_inc(consts_ready, 1)
            nc.gpsimd.iota(rank[:], pattern=[[-1, E]], base=E, channel_multiplier=0,
                           allow_small_or_imprecise_dtypes=True).then_inc(consts_ready, 1)
            pool.wait_ge(consts_ready, 2)
            nc.gpsimd.affine_select(out=ident[:], in_=ident[:], compare_op=ALU.not_equal, fill=1.0, base=0,
                                    pattern=[[-1, P]], channel_multiplier=1).then_inc(consts_ready, 1)
            nc.gpsimd.affine_select(out=causal_bf[:], in_=causal_bf[:], compare_op=ALU.is_ge, fill=-1e30, base=0,
                                    pattern=[[-1, P]], channel_multiplier=1).then_inc(consts_ready, 1)
            pool.wait_ge(consts_ready, 6)
            nc.gpsimd.tensor_copy(ident_bf[:], ident[:]).then_inc(consts_ready, 1)
            for dst, src in ((cent[:], centroids), (bp_col[:], bp), (b1_sb[:], b1), (b2_sb[:], b2),
                             (router_w[:, 0:D], wp), (lat_cur[:, 0, :], wp_t), (lat_cur[:, 1, :], w_down)):
                pool.dma_start(dst, src).then_inc(small_loaded, 16)

        ROOT_LN, ROOT_CENT, ROOT_ROUTE = (0, 4, 5), 1, (2, 6)
        SMALL = 7 * 16
        CONSTS = 7

        def run_slots(eng, slot):
            for i in range(-4, HEADS + 1):
                slot(0, i, lambda u: u >= 0)
            with eng.Fori(1, BATCH - 1) as b:
                for i in range(1, HEADS + 1):
                    slot(b, i, lambda u: True)
            for i in range(1, HEADS + 3):
                slot(BATCH - 1, i, lambda u: u < HEADS)

        @block.tensor
        def _(pe):
            for own in (xt_ready, prep_mm, route_mm, lat_mm, l1_done, l2_done, combT_done, accT_done, q_done,
                      s_done, t_done, z_done, o_done, oT_done):
                pe.sem_inc(own, CREDIT)
            pe.wait_ge(consts_ready, CONSTS)

            def split_mm(dst, w_hi, w_lo, m_hi, m_lo, start=True, stop=True):
                nc.tensor.matmul(dst, w_hi, m_hi, start=start, stop=False)
                nc.tensor.matmul(dst, w_hi, m_lo, start=False, stop=False)
                return nc.tensor.matmul(dst, w_lo, m_hi, start=False, stop=stop)

            def transpose_x(k):
                for g in range(GROUPS):
                    n = k * GROUPS + g
                    pe.wait_ge(norm_done, did(n + 1))
                    pe.wait_ge(xlo_done, did(n - 1))
                    for i in range(GROUP):
                        last = nc.tensor.transpose(bank[g % 2][:, i * P:(i + 1) * P], xn[:, g * GROUP + i, :], ident[:])
                    last.then_inc(xt_ready, 1)

            def prepare_router():
                pe.wait_ge(small_loaded, SMALL)
                pe.wait_ge(r_done, did(1))
                nc.tensor.transpose(bank[7][:, 0:E], cent[:], ident[0:E, 0:E]).then_inc(prep_mm, 1)
                pe.wait_ge(r_done, did(2))
                nc.tensor.matmul(bank[6][:, 0:E], ones[:].broadcast_to([P, P]), cent_sq[:], start=True, stop=True)
                nc.tensor.matmul(bank[6][:, P:P + E], lat_cur[:, 0, :], cent_t[:], start=True, stop=True)
                bp_wide = bp_col[:].broadcast_to([P, P])
                nc.tensor.matmul(bank[6][:, 2 * P:3 * P], bp_wide, ident[:], start=True, stop=True)
                nc.tensor.matmul(bank[6][:, 3 * P:3 * P + E], bp_wide, cent_t[:], start=True, stop=True) \
                    .then_inc(prep_mm, 1)

            def route(f):
                pe.wait_ge(r_done, did(3))
                for n in range(TILES // 2):
                    pe.wait_ge(xlo_done, did((2 * f) * GROUPS + n // 2 + 1))
                    pe.wait_ge(r_done, did(3 + f * (TILES // 2) + n - 3))
                    for j in range(2):
                        i = 2 * n + j
                        last = nc.tensor.matmul(bank[2 + n % 4][:, j * R_COLS:(j + 1) * R_COLS], xT[:, i * P:(i + 1) * P],
                                                router_w[:], start=True, stop=True)
                    last.then_inc(route_mm, 1)

            def prepare_attention():
                for k in range(AB):
                    for slot in range(2):
                        pe.wait_ge(staged[slot], 16 * (W_CHUNKS // 2 + k + 1))
                    pe.wait_ge(w_done, did(W_CHUNKS + k))
                    for h in range(HH):
                        last = nc.tensor.matmul(pair[3][:, h * D:(h + 1) * D], stage[0][0:HD, h * D:(h + 1) * D],
                                                stage[1][0:HD, h * D:(h + 1) * D], start=True, stop=True)
                    last.then_inc(prep_mm, 1)

            def experts(f):
                pe.wait_ge(comb_ready, did(f + 1))
                pe.wait_ge(w_done, did(W_CHUNKS))

                def layer1(t, s):
                    e, c = s // FC, s % FC
                    pe.wait_ge(gelu_done, did(base + t * STEPS + s - 1))
                    w_hi, w_lo = (w[:, e, c * P:(c + 1) * P] for w in (w1_hi, w1_lo))
                    dst = h_ps[s % 2]
                    for w, m, first, end in ((w_hi, xhi, True, False), (w_hi, xlo, False, False), (w_lo, xhi, False, True)):
                        for j in range(2):
                            last = nc.tensor.matmul(dst[:, j * HALF:(j + 1) * HALF], w,
                                                    m[:, bass.ds(t * WIDE + j * HALF, HALF)], start=first, stop=end)
                    last.then_inc(l1_done, 1)

                def comb_rows(t, e):
                    g = (base // STEPS) * E + t * E + e
                    pe.wait_ge(combs_done, did(g))
                    for i in range(WT):
                        last = nc.tensor.transpose(c_ps[:, i * P:(i + 1) * P],
                                                   comb_cur[:, i, e:e + 1].broadcast_to([P, P]), ident[:])
                    last.then_inc(combT_done, 1)

                def layer2(t, s):
                    e, c = s // FC, s % FC
                    g = (base // STEPS) * E + t * E + e
                    pe.wait_ge(gelu_done, did(base + t * STEPS + s + 1))
                    if c == 0:
                        pe.wait_ge(one_done, did(g))
                    w_hi, w_lo = (w[:, e, c, :] for w in (w2_hi, w2_lo))
                    for n, (w, m) in enumerate(((w_hi, ring_hi), (w_lo, ring_hi), (w_hi, ring_lo))):
                        if n == 2:
                            pe.wait_ge(lo_done, did(base + t * STEPS + s + 1))
                        for j in range(2):
                            last = nc.tensor.matmul(y_ps[:, j * HALF:(j + 1) * HALF], w, m[:, s % 2, j * HALF:(j + 1) * HALF],
                                                    start=c == 0 and n == 0, stop=c == FC - 1 and n == 2)
                    last.then_inc(l2_done, 1)

                base = f * PASSES * STEPS
                with pe.Fori(0, PASSES) as t:
                    pe.wait_ge(xup_done, did(f * PASSES + t))
                    pe.wait_ge(combcur_done, did(f * PASSES + t + 1))
                    layer1(t, 0)
                    for s in range(STEPS):
                        if s + 1 < STEPS:
                            layer1(t, s + 1)
                        if s % FC == 0:
                            comb_rows(t, s // FC)
                        layer2(t, s)
                    pe.wait_ge(acc_done, did((f * PASSES + t + 1) * (E - 1)))
                    for i in range(WT):
                        last = nc.tensor.transpose(c_ps[:, i * P:(i + 1) * P], y_acc[:, i * P:(i + 1) * P], ident[:])
                    last.then_inc(accT_done, 1)

            def latents():
                w = lat_cur[:, 1, :]
                for g in range(GROUPS):
                    pe.wait_ge(xlo_done, did(GROUPS + g + 1))
                    pe.wait_ge(lat_done, did(g - 1))
                    nc.tensor.matmul(bank[2 + 2 * (g % 2)], w, xT[:, g * HALF:(g + 1) * HALF], start=True, stop=True)
                    for i in range(GROUP):
                        n = g * GROUP + i
                        last = nc.tensor.matmul(bank[3 + 2 * (g % 2)][:, i * P:(i + 1) * P], xT[:, n * P:(n + 1) * P], w,
                                                start=True, stop=True)
                    last.then_inc(lat_mm, 1)

            def attention_slot(b0, i, live):
                def unit(u):
                    return b0 * HEADS + u, u % HEADS, b0 + u // HEADS
                if live(i + 3):
                    n, h, b = unit(i + 3)
                    pe.wait_ge(qev_done, did(n + 1))
                    pe.wait_ge(exp_done, did(n - 1))
                    dst, q = s_bank[(i + 3) % 2], q_ring[(i + 3) % 2]
                    nc.tensor.matmul(dst[:, P:PC], q[:, P:SEQ], lat_T[:, bass.ds(b * SEQ, SEQ)], start=True, stop=False,
                                     skip_group_check=True)
                    nc.tensor.matmul(dst[:, 0:P], q[:, 0:P], lat_T[:, bass.ds(b * SEQ, P)], start=False, stop=False,
                                     skip_group_check=True)
                    nc.tensor.matmul(dst[:, 0:P], ident_bf[:], causal_bf[:], start=False, stop=False,
                                     skip_group_check=True)
                    nc.tensor.matmul(dst[:, 2 * P:PC], ident_bf[:], causal_bf[:], start=False, stop=True,
                                     skip_group_check=True).then_inc(s_done, 1)
                if i % HEADS == 2 and live(i - 3):
                    n, _, b = unit(i - 3)
                    pe.wait_ge(oev_done, did(b + 1))
                    pe.wait_ge(qev_done, did(n + 7 if live(i + 3) else UNITS))
                    for j in range(QT):
                        last = nc.tensor.transpose(q_bank[:, j * P:(j + 1) * P], o_sb[:, j * P:(j + 1) * P], ident[:])
                    last.then_inc(oT_done, 1)
                if live(i + 4):
                    n, h, b = unit(i + 4)
                    pe.wait_ge(qev_done, did(n))
                    if i % HEADS == 2 and live(i - 3):
                        pe.wait_ge(xres_done, did(b))
                    m = [m[:, bass.ds(b * SEQ, SEQ)] for m in (xhi, xlo)]
                    split_mm(q_bank[:, 0:SEQ], a_hi[:, h, :], a_lo[:, h, :], m[0], m[1]).then_inc(q_done, 1)
                if live(i + 1):
                    n, h, b = unit(i + 1)
                    pe.wait_ge(pn_done, did(n + 1))
                    pe.wait_ge(pt_done, did(n - 1))
                    for dst, src in ((0, 0), (1, 1), (2, 2)):
                        last = nc.tensor.transpose(t_bank[(i + 1) % 2][:, dst * P:(dst + 1) * P],
                                                   p_ring[(i + 1) % 2][:, src * P:(src + 1) * P], ident[:])
                    last.then_inc(t_done, 1)
                if live(i):
                    n, h, b = unit(i)
                    pe.wait_ge(pt_done, did(n + 1))
                    pe.wait_ge(zlo_done, did(n - 1))
                    if h == 0:
                        pe.wait_ge(latcur_done, did(b + 1))
                    z, pt = z_bank[i % 2], pt_ring[i % 2]
                    nc.tensor.matmul(z[:, 0:SEQ], lat_cur[:, 0, :], pt[:, 0:SEQ], start=True, stop=False)
                    nc.tensor.matmul(z[:, P:SEQ], lat_cur[:, 1, :], pt[:, SEQ:PC], start=False, stop=True) \
                        .then_inc(z_done, 1)
                if live(i - 1):
                    n, h, b = unit(i - 1)
                    pe.wait_ge(zlo_done, did(n + 1))
                    if h == 0:
                        pe.wait_ge(oev_done, did(b))
                    k = (i - 1) % 2
                    split_mm(o_bank[:, 0:SEQ], b_hi[:, h, :], b_lo[:, h, :], ring_hi[:, k, 0:SEQ], ring_lo[:, k, 0:SEQ],
                             start=h == 0, stop=h == HEADS - 1).then_inc(o_done, 1)

            transpose_x(0)
            prepare_router()
            route(0)
            prepare_attention()
            experts(0)
            transpose_x(1)
            latents()
            run_slots(pe, attention_slot)
            transpose_x(2)
            route(1)
            experts(1)

        @block.scalar
        def _(act):
            for own in (sqrt_done, xhi_done, gelu_done, exp_done, pt_done, zhi_done, wsplit_hi):
                act.sem_inc(own, CREDIT)

            def root(r, dst, src):
                act.wait_ge(root_in, did(r + 1))
                nc.scalar.activation(dst, src, ACT.Sqrt).then_inc(sqrt_done, 1)

            def layernorm(k):
                root(ROOT_LN[k], std[:], rstd[:])
                for g in range(GROUPS):
                    act.wait_ge(xt_ready, did(k * GROUPS + g + 1))
                    nc.scalar.activation(xhi[:, g * HALF:(g + 1) * HALF], bank[g % 2], ACT.Copy) \
                        .then_inc(xhi_done, 1)

            def split_weights():
                half = W_CHUNKS // 2
                for k in range(W_CHUNKS):
                    act.wait_ge(staged[k % 2], 16 * (k // 2 + 1))
                    dst = (w1_hi[:], w2_hi[:].rearrange("p e c d -> p e (c d)"))[k // half].rearrange("p e n -> p (e n)")
                    nc.scalar.activation(dst[:, (k % half) * WIDE:(k % half + 1) * WIDE], stage[k % 2], ACT.Copy) \
                        .then_inc(wsplit_hi, 1)

            def split_attention():
                for k in range(AB):
                    act.wait_ge(prep_mm, did(2 + k + 1))
                    dst = (a_hi, b_hi)[k // 2][:, (k % 2) * HH:(k % 2 + 1) * HH, :].rearrange("p h d -> p (h d)")
                    nc.scalar.activation(dst, pair[3][:], ACT.Copy, scale=(HD ** -0.5, 1.0)[k // 2]) \
                        .then_inc(wsplit_hi, 1)

            def router_roots(f):
                root(ROOT_ROUTE[f], tok_s[:, 1, :], tok_s[:, 0, :])
                root(ROOT_ROUTE[f] + 1, r_buf[4], r_buf[3])

            def experts(f):
                act.wait_ge(comb_ready, did(f + 1))
                with act.Fori(0, PASSES) as t:
                    for s in range(STEPS):
                        e, c = s // FC, s % FC
                        n = f * PASSES * STEPS + t * STEPS + s
                        act.wait_ge(l1_done, did(n + 1))
                        act.wait_ge(lo_done, did(n - 1))
                        nc.scalar.activation(h_ring[:, s % 2, :], h_ps[s % 2][:], ACT.Gelu, bias=b1_sb[:, e, c:c + 1])
                        act.wait_ge(l2_done, did(n - 1))
                        nc.scalar.activation(ring_hi[:, s % 2, :], h_ps[s % 2][:], ACT.Gelu, bias=b1_sb[:, e, c:c + 1]) \
                            .then_inc(gelu_done, 1)

            def attention_slot(b0, i, live):
                def unit(u):
                    return b0 * HEADS + u
                if live(i - 1):
                    n, k = unit(i - 1), (i - 1) % 2
                    act.wait_ge(z_done, did(n + 1))
                    act.wait_ge(o_done, did(n - 1))
                    nc.scalar.activation(ring_hi[:, k, 0:SEQ], z_bank[k][:, 0:SEQ], ACT.Copy).then_inc(zhi_done, 1)
                if live(i + 1):
                    n, k = unit(i + 1), (i + 1) % 2
                    act.wait_ge(t_done, did(n + 1))
                    act.wait_ge(z_done, did(n - 1))
                    nc.scalar.activation(pt_ring[k], t_bank[k][:, 0:PC], ACT.Copy).then_inc(pt_done, 1)
                if live(i + 3):
                    n, k = unit(i + 3), (i + 3) % 2
                    act.wait_ge(max_done, did(n + 1))
                    act.wait_ge(t_done, did(n - 1))
                    nc.scalar.activation(p_ring[k][:, 0:P], s_bank[k][:, 0:P], ACT.Exp, bias=neg_max[:, k, 0:1],
                                         accum_out=row_sum[:, k, 0:1])
                    nc.scalar.activation(p_ring[k][:, P:PC], s_bank[k][:, P:PC], ACT.Exp, bias=neg_max[:, k, 1:2],
                                         accum_out=row_sum[:, k, 1:2]).then_inc(exp_done, 1)

            layernorm(0)
            root(ROOT_CENT, cent_s[:, 1:2], cent_s[:, 0:1])
            split_weights()
            router_roots(0)
            split_attention()
            act.wait_ge(small_loaded, SMALL)
            experts(0)
            layernorm(1)
            run_slots(act, attention_slot)
            layernorm(2)
            router_roots(1)
            experts(1)

        @block.vector
        def _(dve):
            for own in (dve_chain, root_in, norm_done, xlo_done, w_done, r_done, lat_done, combcur_done,
                      comb_ready, lo_done, combs_done, one_done, acc_done, xup_done,
                      qev_done, max_done, rec_done, pn_done, zlo_done, latcur_done,
                      oev_done, xres_done):
                dve.sem_inc(own, CREDIT)
            chain = [0]

            def link(instruction):
                chain[0] += 1
                instruction.then_inc(dve_chain, 1)
                dve.wait_ge(dve_chain, did(chain[0]))

            V = nc.vector

            def layernorm(k):
                for i in range(TILES):
                    if k == 0 and i % (TILES // 4) == 0:
                        dve.wait_ge(x_loaded[i // (TILES // 4)], 16)
                    last = V.bn_stats(stats[:, i, :], x_tok[:, i, :])
                link(last)
                for i in range(TILES):
                    last = V.bn_aggr(mean_var[:, i, :], stats[:, i, :])
                link(last)
                V.tensor_scalar(rstd[:], mean_var[:, :, 1], LN_EPS, None, ALU.add).then_inc(root_in, 1)
                dve.wait_ge(sqrt_done, did(ROOT_LN[k] + 1))
                a, b = tok_s[:, 0, :], tok_s[:, 1, :]
                link(V.reciprocal(a, std[:]))
                link(V.tensor_tensor(b, a, rstd[:], ALU.mult))
                link(V.tensor_tensor(a, b, std[:], ALU.add))
                link(V.tensor_scalar(b, a, 0.5, None, ALU.mult))
                link(V.reciprocal(rstd[:], b))
                for g in range(GROUPS):
                    for i in range(g * GROUP, (g + 1) * GROUP):
                        last = V.tensor_scalar(xn[:, i, :], x_tok[:, i, :], mean_var[:, i, 0:1], rstd[:, i:i + 1],
                                               ALU.subtract, ALU.mult)
                    last.then_inc(norm_done, 1)
                for g in range(GROUPS):
                    n, cols = k * GROUPS + g, slice(g * HALF, (g + 1) * HALF)
                    dve.wait_ge(xhi_done, did(n + 1))
                    link(V.tensor_copy(xT[:, cols], bank[g % 2]))
                    V.tensor_tensor(xlo[:, cols], xT[:, cols], xhi[:, cols].bitcast(F32), ALU.subtract) \
                        .then_inc(xlo_done, 1)

            def scale_to_ball(scale, norm):
                link(V.tensor_scalar(scale, norm, BALL_EPS, None, ALU.max))
                link(V.reciprocal(scale, scale))
                link(V.tensor_scalar(scale, scale, MAX_NORM, 1.0, ALU.mult, ALU.min))

            def prepare_router():
                dve.wait_ge(small_loaded, SMALL)
                link(V.tensor_tensor(comb_cur[0:E, :, :].rearrange("p a b -> p (a b)"), cent[:, 0:D // 2], cent[:, 0:D // 2], ALU.mult))
                link(V.tensor_reduce(cent_s[:, 2:3], comb_cur[0:E, :, :].rearrange("p a b -> p (a b)"), AX.X, ALU.add))
                link(V.tensor_tensor(comb_cur[0:E, :, :].rearrange("p a b -> p (a b)"), cent[:, D // 2:D], cent[:, D // 2:D], ALU.mult))
                link(V.tensor_reduce(cent_s[:, 3:4], comb_cur[0:E, :, :].rearrange("p a b -> p (a b)"), AX.X, ALU.add))
                V.tensor_tensor(cent_s[:, 0:1], cent_s[:, 2:3], cent_s[:, 3:4], ALU.add).then_inc(root_in, 1)
                dve.wait_ge(sqrt_done, did(ROOT_CENT + 1))
                scale_to_ball(cent_s[:, 2:3], cent_s[:, 1:2])
                V.tensor_scalar(cent[:], cent[:], cent_s[:, 2:3], None, ALU.mult).then_inc(r_done, 1)
                dve.wait_ge(prep_mm, did(1))
                link(V.tensor_copy(cent_t[:], bank[7][:, 0:E]))
                V.tensor_tensor(cent_sq[:], cent_t[:], cent_t[:], ALU.mult).then_inc(r_done, 1)
                dve.wait_ge(prep_mm, did(2))
                link(V.tensor_scalar(cn2[:, 0, :], bank[6][:, 0:E], MAX_SQ, None, ALU.min))
                V.tensor_scalar(cn2[:, 1, :], cn2[:, 0, :], -1.0, 1.0, ALU.mult, ALU.add)
                V.tensor_copy(router_w[:, D:R_COLS], bank[6][:, P:P + E])
                V.tensor_copy(router_b[:], bank[6][:, 2 * P:2 * P + R_COLS]).then_inc(r_done, 1)

            def split_weights():
                half = W_CHUNKS // 2
                for k in range(W_CHUNKS):
                    dve.wait_ge(wsplit_hi, did(k + 1))
                    cols = slice((k % half) * WIDE, (k % half + 1) * WIDE)
                    hi, lo = (w.rearrange("p e n -> p (e n)")[:, cols] for w in (
                        (w1_hi[:], w1_lo[:]) if k < half else
                        (w.rearrange("p e c d -> p e (c d)") for w in (w2_hi[:], w2_lo[:]))))
                    V.tensor_tensor(lo, stage[k % 2], hi.bitcast(F32), ALU.subtract).then_inc(w_done, 1)

            def split_attention():
                for k in range(AB):
                    dve.wait_ge(wsplit_hi, did(W_CHUNKS + k + 1))
                    hi, lo = (w[:, (k % 2) * HH:(k % 2 + 1) * HH, :].rearrange("p h d -> p (h d)")
                              for w in ((a_hi, a_lo), (b_hi, b_lo))[k // 2])
                    V.scalar_tensor_tensor(lo, pair[3][:], (HD ** -0.5, 1.0)[k // 2], hi.bitcast(F32),
                                           ALU.mult, ALU.subtract).then_inc(w_done, 1)

            def route(f):
                def per_token(j):
                    return tok_s[:, j, :].unsqueeze(2).broadcast_to([P, TILES, E])

                def per_expert(v):
                    return v.unsqueeze(1).broadcast_to([P, TILES, E])

                for n in range(TILES // 2):
                    dve.wait_ge(route_mm, did(f * (TILES // 2) + n + 1))
                    got = bank[2 + n % 4][:, 0:2 * R_COLS].rearrange("p (t c) -> p t c", t=2)
                    V.tensor_tensor(xn[:, 2 * n:2 * n + 2, :], got[:, :, 0:D],
                                    router_b[:, 0:D].unsqueeze(1).broadcast_to([P, 2, D]), ALU.add)
                    V.tensor_tensor(r_dot[:, 2 * n:2 * n + 2, :], got[:, :, D:R_COLS],
                                    router_b[:, D:R_COLS].unsqueeze(1).broadcast_to([P, 2, E]), ALU.add) \
                        .then_inc(r_done, 1)
                dve.wait_ge(r_done, did(3 + (f + 1) * (TILES // 2)))
                link(V.tensor_tensor(xn[:], xn[:], xn[:], ALU.mult))
                V.tensor_reduce(tok_s[:, 0, :], xn[:], AX.X, ALU.add).then_inc(root_in, 1)
                dve.wait_ge(sqrt_done, did(ROOT_ROUTE[f] + 1))
                scale_to_ball(tok_s[:, 2, :], tok_s[:, 1, :])
                link(V.tensor_tensor(tok_s[:, 3, :], tok_s[:, 2, :], tok_s[:, 2, :], ALU.mult))
                link(V.tensor_tensor(tok_s[:, 3, :], tok_s[:, 3, :], tok_s[:, 0, :], ALU.mult))
                link(V.tensor_scalar(tok_s[:, 3, :], tok_s[:, 3, :], MAX_SQ, None, ALU.min))
                link(V.tensor_scalar(tok_s[:, 4, :], tok_s[:, 3, :], -1.0, 1.0, ALU.mult, ALU.add))
                dot, arg, den, under, rt, sel1, sel2, tmp = r_buf
                link(V.tensor_tensor(dot, r_dot[:], per_token(2), ALU.mult))
                link(V.scalar_tensor_tensor(arg, dot, -2.0, per_expert(cn2[:, 0, :]), ALU.mult, ALU.add))
                link(V.tensor_tensor(arg, arg, per_token(3), ALU.add))
                link(V.tensor_tensor(den, per_expert(cn2[:, 1, :]), per_token(4), ALU.mult))
                link(V.tensor_scalar(den, den, BALL_EPS, None, ALU.add))
                link(V.reciprocal(den, den))
                link(V.scalar_tensor_tensor(arg, arg, 0.0, den, ALU.max, ALU.mult))
                link(V.tensor_scalar(arg, arg, 2.0, 1.0, ALU.mult, ALU.add))
                link(V.tensor_scalar(arg, arg, 1.0 + BALL_EPS, None, ALU.max))
                link(V.tensor_scalar(under, arg, 1.0, None, ALU.add))
                V.scalar_tensor_tensor(under, arg, -1.0, under, ALU.add, ALU.mult).then_inc(root_in, 1)
                dve.wait_ge(sqrt_done, did(ROOT_ROUTE[f] + 2))
                link(V.tensor_tensor(arg, arg, rt, ALU.add))
                u = dot
                link(V.reciprocal(u, arg))

                def best(sel, m, k):
                    link(V.tensor_reduce(tok_s[:, m, :], u, AX.X, ALU.max))
                    link(V.tensor_tensor(tmp, u, per_token(m), ALU.is_equal))
                    link(V.tensor_tensor(tmp, tmp, per_expert(rank[:]), ALU.mult))
                    link(V.tensor_reduce(tok_s[:, k, :], tmp, AX.X, ALU.max))
                    link(V.tensor_tensor(sel, tmp, per_token(k), ALU.is_equal))

                best(sel1, 5, 0)
                link(V.scalar_tensor_tensor(u, sel1, -2.0, u, ALU.mult, ALU.add))
                best(sel2, 6, 0)
                link(V.reciprocal(tok_s[:, 5, :], tok_s[:, 5, :]))
                link(V.tensor_tensor(tok_s[:, 6, :], tok_s[:, 6, :], tok_s[:, 5, :], ALU.mult))
                link(V.tensor_scalar(tok_s[:, 5, :], tok_s[:, 6, :], 1.0, None, ALU.add))
                link(V.reciprocal(tok_s[:, 5, :], tok_s[:, 5, :]))
                link(V.tensor_tensor(tok_s[:, 6, :], tok_s[:, 6, :], tok_s[:, 5, :], ALU.mult))
                link(V.tensor_tensor(sel1, sel1, per_token(5), ALU.mult))
                link(V.tensor_tensor(sel2, sel2, per_token(6), ALU.mult))
                V.tensor_tensor(comb[:], sel1, sel2, ALU.add).then_inc(comb_ready, 1)
                dve.wait_ge(comb_ready, did(f + 1))

            def experts(f):
                def fold(p, s_next, e):
                    g = p * E + e
                    dve.wait_ge(l2_done, did(s_next))
                    dve.wait_ge(combs_done, did(g + 1))
                    if e > 1:
                        dve.wait_ge(acc_done, did(p * (E - 1) + e - 1))
                    V.scalar_tensor_tensor(y_acc if e == 0 else y_one, y_ps[:], b2_sb[:, e:e + 1], comb_b[:, e % 2, :],
                                           ALU.add, ALU.mult).then_inc(one_done, 1)
                    if e > 0:
                        dve.wait_ge(one_done, did(g + 1))
                        V.tensor_tensor(y_acc, y_acc, y_one, ALU.add).then_inc(acc_done, 1)

                with dve.Fori(0, PASSES) as t:
                    p = f * PASSES + t
                    dve.wait_ge(combT_done, did(p * E))
                    V.tensor_copy(comb_cur[:], comb[:, bass.ds(t * WT, WT), :]).then_inc(combcur_done, 1)
                    for s in range(STEPS):
                        e, n = s // FC, p * STEPS + s
                        dve.wait_ge(gelu_done, did(n + 1))
                        dve.wait_ge(l2_done, did(n - 1))
                        V.tensor_tensor(ring_lo[:, s % 2, :], h_ring[:, s % 2, :], ring_hi[:, s % 2, :].bitcast(F32),
                                        ALU.subtract).then_inc(lo_done, 1)
                        if s % FC == 0:
                            if e > 0:
                                fold(p, n, e - 1)
                            dve.wait_ge(combT_done, did(p * E + e + 1))
                            V.tensor_copy(comb_b[:, e % 2, :], c_ps[:]).then_inc(combs_done, 1)
                    fold(p, (p + 1) * STEPS, E - 1)
                    dve.wait_ge(accT_done, did(p + 1))
                    here = x_tok[:].rearrange("p t d -> p (t d)")[:, bass.ds(t * WIDE, WIDE)]
                    V.scalar_tensor_tensor(here, c_ps[:], 0.5, here, ALU.mult, ALU.add).then_inc(xup_done, 1)
                dve.wait_ge(xup_done, did((f + 1) * PASSES))

            def latents():
                for g in range(GROUPS):
                    dve.wait_ge(lat_mm, did(g + 1))
                    V.tensor_copy(lat_T[:, g * HALF:(g + 1) * HALF], bank[2 + 2 * (g % 2)])
                    V.tensor_copy(lat_tok[:, g * GROUP:(g + 1) * GROUP, :].rearrange("p t d -> p (t d)"),
                                  bank[3 + 2 * (g % 2)]).then_inc(lat_done, 1)
                dve.wait_ge(lat_done, did(GROUPS))

            def attention_slot(b0, i, live):
                def unit(u):
                    return b0 * HEADS + u, b0 + u // HEADS
                if i % HEADS == 0 and live(i):
                    n, b = unit(i)
                    dve.wait_ge(z_done, did(n))
                    V.tensor_copy(lat_cur[:], lat_tok[:, bass.ds(b * QT, QT), :]).then_inc(latcur_done, 1)
                if live(i + 2):
                    n, k = unit(i + 2)[0], (i + 2) % 2
                    dve.wait_ge(exp_done, did(n + 1))
                    link_slot(V.reciprocal(row_rec[:, k, :], row_sum[:, k, :]), n)
                    for j, cols in ((0, slice(0, P)), (1, slice(P, PC))):
                        last = V.tensor_scalar(p_ring[k][:, cols], p_ring[k][:, cols], row_rec[:, k, j:j + 1], None, ALU.mult)
                    last.then_inc(pn_done, 1)
                if live(i - 1):
                    n, k = unit(i - 1)[0], (i - 1) % 2
                    dve.wait_ge(zhi_done, did(n + 1))
                    dve.wait_ge(o_done, did(n - 1))
                    V.tensor_tensor(ring_lo[:, k, 0:SEQ], z_bank[k][:, 0:SEQ], ring_hi[:, k, 0:SEQ].bitcast(F32),
                                    ALU.subtract).then_inc(zlo_done, 1)
                if i % HEADS == 1 and live(i - 2):
                    n, b = unit(i - 2)
                    dve.wait_ge(o_done, did(n + 1))
                    dve.wait_ge(oT_done, did(b))
                    V.tensor_copy(o_sb, o_bank[:, 0:SEQ]).then_inc(oev_done, 1)
                if live(i + 3):
                    n, k = unit(i + 3)[0], (i + 3) % 2
                    dve.wait_ge(s_done, did(n + 1))
                    dve.wait_ge(exp_done, did(n - 1))
                    V.tensor_reduce(neg_max[:, k, 0:1], s_bank[k][:, 0:P], AX.X, ALU.max, negate=True)
                    V.tensor_reduce(neg_max[:, k, 1:2], s_bank[k][:, P:PC], AX.X, ALU.max, negate=True) \
                        .then_inc(max_done, 1)
                if i % HEADS == 2 and live(i - 3):
                    n, b = unit(i - 3)
                    dve.wait_ge(oT_done, did(b + 1))
                    here = x_tok[:].rearrange("p t d -> p (t d)")[:, bass.ds(b * SEQ, SEQ)]
                    V.tensor_tensor(here, here, q_bank[:, 0:SEQ], ALU.add).then_inc(xres_done, 1)
                if live(i + 4):
                    n, k = unit(i + 4)[0], i % 2
                    dve.wait_ge(q_done, did(n + 1))
                    dve.wait_ge(s_done, did(n - 1))
                    V.tensor_copy(q_ring[k], q_bank[:, 0:SEQ]).then_inc(qev_done, 1)

            def link_slot(instruction, n):
                instruction.then_inc(rec_done, 1)
                dve.wait_ge(rec_done, did(n + 1))

            layernorm(0)
            prepare_router()
            split_weights()
            route(0)
            split_attention()
            experts(0)
            layernorm(1)
            latents()
            run_slots(dve, attention_slot)
            dve.wait_ge(xres_done, did(BATCH))
            layernorm(2)
            route(1)
            experts(1)
    return nc


_OUT = (16, 256, 128)


def kernel(**inputs):
    import numpy as _np
    import concourse.bacc as _bacc
    from concourse import mybir as _mybir
    from concourse.bass_utils import run_bass_kernel_spmd as _run

    a = {k: _np.asarray(v) for k, v in inputs.items()}
    C = a["L0_attn_x"].shape[-1]
    E, _, F = a["L0_ffn_W1"].shape
    HD = 64
    HEADS = a["L0_attn_w_q"].shape[1] // HD
    up = a["L0_attn_w_kv_up"]
    cut = HEADS * HD
    laid = {
        "x": a["L0_attn_x"],
        "w_down": a["L0_attn_w_kv_down"],
        "wq_t": a["L0_attn_w_q"].T.reshape(HEADS, HD, C).transpose(1, 0, 2),
        "wuk_t": up[:, :cut].T.reshape(HEADS, HD, C).transpose(1, 0, 2),
        "wuv_t": up[:, cut:].T.reshape(HEADS, HD, C).transpose(1, 0, 2),
        "w_out": a["L0_attn_w_out"].reshape(HEADS, HD, C).transpose(1, 0, 2),
        "centroids": a["L0_ffn_centroids"],
        "wp_t": a["L0_ffn_Wp"].T,
        "wp": a["L0_ffn_Wp"],
        "bp": a["L0_ffn_bp"].reshape(C, 1),
        "w1": a["L0_ffn_W1"].transpose(1, 0, 2),
        "b1": a["L0_ffn_b1"].reshape(E, F // 128, 128).transpose(2, 0, 1),
        "w2": a["L0_ffn_W2"].reshape(E, F // 128, 128, C).transpose(2, 0, 1, 3).reshape(128, E, F // 128 * C),
        "b2": a["L0_ffn_b2"].T,
    }
    nc = _bacc.Bacc("TRN2", target_bir_lowering=False, num_devices=1)
    arrays, args = {}, []
    for name, v in laid.items():
        v = _np.ascontiguousarray(v)
        arrays[f"in_{name}"] = v
        args.append(nc.dram_tensor(f"in_{name}", v.shape, _mybir.dt.from_np(v.dtype), kind="ExternalInput").ap())
    out = nc.dram_tensor("out", _OUT, _mybir.dt.float32, kind="ExternalOutput").ap()
    macaron_block(nc, *args, out)
    r = _run(nc, [arrays], core_ids=[0])
    return r.results[0]["out"]
```

```python
import concourse.bass as bass
from concourse import mybir
from contextlib import ExitStack

F32 = mybir.dt.float32
F32R = mybir.dt.float32r
BF16 = mybir.dt.bfloat16
ALU = mybir.AluOpType
ACT = mybir.ActivationFunctionType
AX = mybir.AxisListType

P = 128
CREDIT = 2


def macaron_block(nc, x, w_down, wq_t, wuk_t, wuv_t, w_out, centroids, wp_t, wp, bp, w1, b1, w2, b2, out):
    BATCH, SEQ, D = x.shape
    HD, HEADS, _ = wq_t.shape
    E, FC = w1.shape[1], w1.shape[2] // P
    TOKENS = BATCH * SEQ
    TILES = TOKENS // P
    QT = SEQ // P
    WT = 8
    WIDE = WT * P
    PASSES = TOKENS // WIDE
    STEPS = E * FC
    UNITS = BATCH * HEADS
    LN_EPS, BALL_EPS, MAX_NORM, MAX_SQ = 1e-5, 1e-7, 0.95, 0.99
    HALF = 512
    R_COLS = D + E
    PC = QT * (QT + 1) // 2 * P
    assert QT == 2 and WIDE == 2 * HALF and FC == 4

    ctx = ExitStack()
    with ctx:
        def sb(name, shape, dt=F32):
            return ctx.enter_context(nc.sbuf_tensor(name, shape, dt))

        def sem(name):
            return ctx.enter_context(nc.semaphore(name))

        x_tok = sb("x_tok", [P, TILES, D])
        x_flat = x_tok[:].rearrange("p t d -> p (t d)")
        xhi = sb("xhi", [P, TOKENS], F32R)
        xlo = sb("xlo", [P, TOKENS], F32R)
        w1_hi = sb("w1_hi", [P, E, FC * P], F32R)
        w1_lo = sb("w1_lo", [P, E, FC * P], F32R)
        w2_hi = sb("w2_hi", [P, E, FC * D], F32R)
        w2_lo = sb("w2_lo", [P, E, FC * D], F32R)
        a_hi = sb("a_hi", [P, HEADS, D], F32R)
        a_lo = sb("a_lo", [P, HEADS, D], F32R)
        b_hi = sb("b_hi", [P, HEADS, D], F32R)
        b_lo = sb("b_lo", [P, HEADS, D], F32R)
        ring_hi = sb("ring_hi", [P, 2, WIDE], F32R)
        ring_lo = sb("ring_lo", [P, 2, WIDE], F32R)
        big = sb("big", [P, 8 * WIDE])
        work = sb("work", [P, 2 * WIDE])
        ident = sb("ident", [P, P])
        ident_bf = sb("ident_bf", [P, P], BF16)
        causal_bf = sb("causal_bf", [P, P], BF16)
        ones = sb("ones", [P, 1])
        powers = sb("powers", [P, 2])
        comb_next = sb("comb_next", [P, E, WT])
        comb_dram = nc.dram_tensor("comb_dram", (E * WT, P), F32).ap()
        r_dot = sb("r_dot", [P, WT, E])
        stats = sb("stats", [P, WT, 6])
        after_wait = sb("after_wait", [P, 1])
        mean_var = sb("mean_var", [P, WT, 2])
        var_eps = sb("var_eps", [P, WT])
        rstd = sb("rstd", [P, WT])
        tok_s = sb("tok_s", [P, 8, WT])
        tok_2 = sb("tok_2", [P, 3, 2, WT])
        router_w = sb("router_w", [P, R_COLS])
        router_b = sb("router_b", [P, R_COLS])
        cent_s = sb("cent_s", [E, 4])
        cent_t = sb("cent_t", [P, E])
        cent_sq = sb("cent_sq", [P, E])
        cn2 = sb("cn2", [P, 2, E])
        rank = sb("rank", [P, E])
        bp_col = sb("bp_col", [P, 1])
        b1_sb = sb("b1_sb", [P, E, FC])
        b2_sb = sb("b2_sb", [P, E])
        w_down_sb = sb("w_down_sb", [P, D])
        lat_cur = sb("lat_cur", [P, QT, P])
        lat_next = sb("lat_next", [P, QT, P])
        neg_max = sb("neg_max", [P, 2, QT])
        row_sum = sb("row_sum", [P, 2, QT])
        row_rec = sb("row_rec", [P, 2, QT])

        def part(k, n=1):
            return big[:, k * WIDE:(k + n) * WIDE]
        h_ring = part(0, 2).rearrange("p (r n) -> p r n", r=2)
        y_acc, y_one = part(2), part(3)
        comb_b = part(4, 2).rearrange("p (r n) -> p r n", r=2)
        lat_T = part(0, 4)
        xn = part(6).rearrange("p (t d) -> p t d", d=D)
        xT = part(7)
        TE = WT * E
        dot, arg, den, sel1, sel2, tmp = (xT[:, k * TE:(k + 1) * TE].rearrange("p (t e) -> p t e", e=E)
                                          for k in range(6))
        comb_T = lat_next[0:E * WT, 1, :]
        wp_t_sb = lat_cur[:, 0, :]
        cent = lat_cur[0:E, 1, :]
        o_sb = sb("o_sb", [P, SEQ])
        stage = [work[:, 0:WIDE], work[:, WIDE:2 * WIDE]] + [part(k) for k in (2, 3, 4, 5)]
        stage += stage[0:2]
        q_ring = [work[:, k * SEQ:(k + 1) * SEQ] for k in range(2)]
        at = 2 * SEQ
        p_ring = [work[:, at + k * PC:at + (k + 1) * PC] for k in range(2)]
        at += 2 * PC
        pt_ring = [work[:, at + k * PC:at + (k + 1) * PC] for k in range(2)]
        at += 2 * PC
        assert at <= 2 * WIDE

        pair = [ctx.enter_context(nc.psum_tensor(f"pair{k}", [P, 2 * HALF], F32)) for k in range(4)]
        h_ps = pair[0:2]
        y_ps = pair[2:4]
        bank = [pair[k // 2][:, (k % 2) * HALF:(k % 2 + 1) * HALF] for k in range(8)]
        q_bank, o_bank = bank[0], bank[1]
        s_bank, t_bank, z_bank = bank[2:4], bank[4:6], bank[6:8]

        small_loaded, x_loaded0, x_loaded, stored = sem("small_loaded"), sem("x_loaded0"), sem("x_loaded"), sem("stored")
        comb_stored = sem("comb_stored")
        comb_loaded = [sem(f"comb_loaded{k}") for k in range(2)]
        ab_staged = sem("ab_staged")
        staged = [sem(f"staged{k}") for k in range(8)]
        consts_ready = sem("consts_ready")
        ln_root, norm_root, arg_root = sem("ln_root"), sem("norm_root"), sem("arg_root")
        wp_done = sem("wp_done")
        acc_done = sem("acc_done")
        xt_ready = sem("xt_ready")
        prep_mm = sem("prep_mm")
        route_mm = sem("route_mm")
        lat_mm = sem("lat_mm")
        l1_done = sem("l1_done")
        hi_used = sem("hi_used")
        l2_done = sem("l2_done")
        combT_mm = sem("combT_mm")
        accT_done = sem("accT_done")
        q_done = sem("q_done")
        s_done = sem("s_done")
        t_done = sem("t_done")
        z_done = sem("z_done")
        o_done = sem("o_done")
        oT_done = sem("oT_done")
        xhi_done = sem("xhi_done")
        gelu_done = sem("gelu_done")
        exp_done = sem("exp_done")
        pt_done = sem("pt_done")
        zhi_done = sem("zhi_done")
        wsplit_hi = sem("wsplit_hi")
        dve_chain = sem("dve_chain")
        ln_in = sem("ln_in")
        norm_in = sem("norm_in")
        arg_in = sem("arg_in")
        norm_done = sem("norm_done")
        xlo_done = sem("xlo_done")
        w_done = sem("w_done")
        rw_done = sem("rw_done")
        r_done = sem("r_done")
        lat_done = sem("lat_done")
        comb_ready = sem("comb_ready")
        combT_done = sem("combT_done")
        lo_done = sem("lo_done")
        one_done = sem("one_done")
        xup_done = sem("xup_done")
        qev_done = sem("qev_done")
        max_done = sem("max_done")
        rec_done = sem("rec_done")
        pn_done = sem("pn_done")
        zlo_done = sem("zlo_done")
        latcur_done = sem("latcur_done")
        oev_done = sem("oev_done")
        xres_done = sem("xres_done")

        def did(n):
            return n + CREDIT

        block = ctx.enter_context(nc.Block())

        SMALL = 7 * 16
        CONSTS = 9
        W_CHUNKS = 8
        HH = HEADS // 2
        AB = 4
        PARTS = WT // QT
        LN_SEQ, LN_PART = PASSES, PASSES + BATCH
        LN_PASS = (0, LN_PART + PARTS - 1)
        AHEAD = 2 * FC
        STEP_STATS, STEP_NORM, STEP_T, STEP_XLO, STEP_R = 9, 11, 14, 15, (18, 22)
        STEP_SQ, STEP_ARGS, STEP_NEAR, STEP_SECOND, STEP_WEIGHTS, STEP_COMB = 23, 25, 26, 27, 29, 31
        AB_STEP = (10, 14, 18, 22)
        SEQ_STATS, SEQ_NORM, SEQ_T, SEQ_XLO = 22, 24, 26, 27
        STEP_SUM, STEP_UPDATE = 2, 3
        PART_STATS, PART_NORM, PART_T, PART_XLO = ([3 * j + k for j in range(PARTS)] for k in (1, 2, 3, 4))
        DVE_CHUNKS, POOL_CHUNKS = (0, 1, 2, 4, 6), (3, 5, 7)
        W_ORDER = [(k % 2, k // 2) for k in range(W_CHUNKS)]

        def last_sequence(b0):
            return isinstance(b0, int) and b0 == BATCH - 1

        def slot_job(stage, b0, i):
            if last_sequence(b0):
                at = (PART_STATS, PART_NORM, PART_T, PART_XLO)[stage]
                return (LN_PART + at.index(i), at.index(i), at.index(i)) if i in at else None
            return (LN_SEQ + b0 + 1, b0 + 1, 0) if i == (3, 5, 6, 7)[stage] else None

        def weight_chunk(k):
            layer, pair_of = W_ORDER[k]
            cols = slice(pair_of * WIDE, (pair_of + 1) * WIDE)
            return [w[:].rearrange("p e n -> p (e n)")[:, cols] for w in ((w1_hi, w1_lo), (w2_hi, w2_lo))[layer]]

        def run_slots(eng, slot):
            for i in range(-4, HEADS + 1):
                slot(0, i, lambda u: u >= 0, i > 0)
            with eng.Fori(1, BATCH - 1) as b:
                for i in range(1, HEADS + 1):
                    slot(b, i, lambda u: True, True)
            for i in range(1, HEADS + 4):
                slot(BATCH - 1, i, lambda u: u < HEADS, True)

        def run_passes(eng, rest_of_pass, f):
            with eng.Fori(0, PASSES - 1) as t:
                rest_of_pass(f, t, True)
            rest_of_pass(f, PASSES - 1, False)

        @block.sync
        def _(sp):
            x_t, out_t = (a.rearrange("b (q p) d -> p (b q) d", p=P) for a in (x, out))
            sp.dma_start(x_tok[:, 0:WT, :], x_t[:, 0:WT, :]).then_inc(x_loaded0, 16)
            for k, (layer, pair_of) in enumerate(W_ORDER):
                if k >= 6:
                    sp.wait_ge(w_done, did(k - 5))
                src = (w1, w2)[layer].rearrange("p e n -> p (e n)")[:, pair_of * WIDE:(pair_of + 1) * WIDE]
                sp.dma_start(stage[k], src).then_inc(staged[k], 16)
            sp.dma_start(x_tok[:, WT:TILES, :], x_t[:, WT:TILES, :]).then_inc(x_loaded, 16)

            def spread_comb(p):
                ready, in_dram = sp.snap(did(p + 1)), sp.snap(16 * (p + 1))
                read = sp.snap(16 * (E // 2) * p + CREDIT)
                free = [sp.snap(did(p * E + e - 1)) for e in range(E)]
                sp.wait_ge(combT_done, ready)
                for k in range(2):
                    sp.wait_ge(comb_loaded[k], read)
                sp.dma_start(comb_dram, comb_T).then_inc(comb_stored, 16)
                sp.wait_ge(comb_stored, in_dram)
                rows = comb_dram.rearrange("(e t) p -> e (t p)", e=E)
                for e in range(E):
                    sp.wait_ge(one_done, free[e])
                    sp.dma_start(comb_b[:, e % 2, :], rows[e:e + 1, :].broadcast_to([P, WIDE])) \
                        .then_inc(comb_loaded[e % 2], 16)

            for k in range(2):
                sp.sem_inc(comb_loaded[k], CREDIT)
            sp.wait_ge(w_done, did(len(DVE_CHUNKS)))
            sp.wait_ge(wp_done, did(len(POOL_CHUNKS)))
            with sp.Fori(0, 2 * PASSES) as p:
                spread_comb(p)


            def store(t):
                sp.wait_ge(xup_done, did(PASSES + t + 1))
                sp.dma_start(out_t[:, t * WT:(t + 1) * WT, :], x_tok[:, t * WT:(t + 1) * WT, :]).then_inc(stored, 16)

            for t in range(PASSES):
                store(t)
            sp.wait_ge(stored, 16 * PASSES)

        @block.gpsimd
        def _(pool):
            for dst, src in ((cent, centroids), (bp_col[:], bp), (b1_sb[:], b1), (b2_sb[:], b2),
                             (router_w[:, 0:D], wp), (wp_t_sb, wp_t), (w_down_sb[:], w_down)):
                pool.dma_start(dst, src).then_inc(small_loaded, 16)
            nc.gpsimd.memset(ident[:], 0.0).then_inc(consts_ready, 1)
            nc.gpsimd.memset(causal_bf[:], 0.0).then_inc(consts_ready, 1)
            nc.gpsimd.memset(ones[:], 1.0).then_inc(consts_ready, 1)
            nc.gpsimd.memset(powers[:, 0:1], -0.5).then_inc(consts_ready, 1)
            nc.gpsimd.memset(powers[:, 1:2], 0.5).then_inc(consts_ready, 1)
            nc.gpsimd.iota(rank[:], pattern=[[-1, E]], base=E, channel_multiplier=0,
                           allow_small_or_imprecise_dtypes=True).then_inc(consts_ready, 1)
            pool.wait_ge(consts_ready, 2)
            nc.gpsimd.affine_select(out=ident[:], in_=ident[:], compare_op=ALU.not_equal, fill=1.0, base=0,
                                    pattern=[[-1, P]], channel_multiplier=1).then_inc(consts_ready, 1)
            nc.gpsimd.affine_select(out=causal_bf[:], in_=causal_bf[:], compare_op=ALU.is_ge, fill=-1e30, base=0,
                                    pattern=[[-1, P]], channel_multiplier=1).then_inc(consts_ready, 1)
            pool.wait_ge(consts_ready, 8)
            nc.gpsimd.tensor_copy(ident_bf[:], ident[:]).then_inc(consts_ready, 1)

            def power(dst, src, which):
                n = src.shape[-1]
                return nc.gpsimd.tensor_tensor(dst, src, powers[0:src.shape[0], which:which + 1].broadcast_to([src.shape[0], n]),
                                               ALU.pow)

            def ln_power(n, tiles):
                pool.wait_ge(ln_in, did(n + 1))
                power(rstd[:, 0:tiles], var_eps[:, 0:tiles], 0).then_inc(ln_root, 1)

            def norm_power(p):
                pool.wait_ge(norm_in, did(1 + p + 1))
                power(tok_s[:, 1, :], tok_s[:, 7, :], 0).then_inc(norm_root, 1)

            def arg_power(p):
                pool.wait_ge(arg_in, did(p + 1))
                power(tok_2[:, 2, :, :].rearrange("p a b -> p (a b)"), tok_2[:, 1, :, :].rearrange("p a b -> p (a b)"), 1) \
                    .then_inc(arg_root, 1)

            def split_weights(k):
                pool.wait_ge(wsplit_hi, did(k + 1))
                hi, lo = weight_chunk(k)
                nc.gpsimd.tensor_tensor(lo, stage[k], hi.bitcast(F32), ALU.subtract).then_inc(wp_done, 1)

            def add(p, e):
                pool.wait_ge(one_done, did(p * E + e + 1))
                nc.gpsimd.tensor_tensor(y_acc, y_acc, y_one, ALU.add).then_inc(acc_done, 1)
                pool.wait_ge(acc_done, did(p * (E - 1) + e))

            def rest_of_pass(f, t, prepare):
                p = f * PASSES + t
                for e in range(1, E):
                    add(p, e)
                    if prepare and e == 1:
                        ln_power(LN_PASS[f] + t + 1, WT)
                    if prepare and e == 4:
                        norm_power(p + 1)
                    if prepare and e == 5:
                        arg_power(p + 1)
                    if f == 0 and not prepare and e == 4:
                        ln_power(LN_SEQ, QT)

            for own in (ln_root, norm_root, arg_root, wp_done, acc_done):
                pool.sem_inc(own, CREDIT)
            ln_power(0, WT)
            pool.wait_ge(norm_in, did(1))
            power(cent_s[:, 1:2], cent_s[:, 0:1], 0).then_inc(norm_root, 1)
            norm_power(0)
            for k in POOL_CHUNKS[0:1]:
                split_weights(k)
            arg_power(0)
            for k in POOL_CHUNKS[1:]:
                split_weights(k)
            run_passes(pool, rest_of_pass, 0)
            with pool.Fori(1, BATCH) as b:
                ln_power(LN_SEQ + b, QT)
            with pool.Fori(0, PARTS) as j:
                ln_power(LN_PART + j, QT)
            norm_power(PASSES)
            arg_power(PASSES)
            run_passes(pool, rest_of_pass, 1)

        @block.tensor
        def _(pe):
            for own in (xt_ready, prep_mm, route_mm, lat_mm, l1_done, hi_used, l2_done, combT_mm, accT_done, q_done,
                        s_done, t_done, z_done, o_done, oT_done):
                pe.sem_inc(own, CREDIT)
            pe.wait_ge(consts_ready, CONSTS)

            def transpose_x(n, dst, tiles, at=0):
                pe.wait_ge(norm_done, did(n + 1))
                for i in range(tiles):
                    last = nc.tensor.transpose(dst[:, i * P:(i + 1) * P], xn[:, at + i, :], ident[:])
                last.then_inc(xt_ready, 1)

            def prepare_router():
                pe.wait_ge(small_loaded, SMALL)
                pe.wait_ge(rw_done, did(1))
                nc.tensor.transpose(bank[5][:, 0:E], cent, ident[0:E, 0:E]).then_inc(prep_mm, 1)
                pe.wait_ge(rw_done, did(2))
                nc.tensor.matmul(bank[4][:, 0:E], ones[:].broadcast_to([P, P]), cent_sq[:], start=True, stop=True)
                nc.tensor.matmul(bank[4][:, P:P + E], wp_t_sb, cent_t[:], start=True, stop=True)
                bp_wide = bp_col[:].broadcast_to([P, P])
                nc.tensor.matmul(bank[4][:, 2 * P:3 * P], bp_wide, ident[:], start=True, stop=True)
                nc.tensor.matmul(bank[4][:, 3 * P:3 * P + E], bp_wide, cent_t[:], start=True, stop=True) \
                    .then_inc(prep_mm, 1)

            def route(half, at):
                for i in range(WT // 2):
                    dst = at[:, (i // 2) * HALF + (i % 2) * R_COLS:(i // 2) * HALF + (i % 2 + 1) * R_COLS]
                    n = half * (WT // 2) + i
                    last = nc.tensor.matmul(dst, xT[:, n * P:(n + 1) * P], router_w[:], start=True, stop=True)
                last.then_inc(route_mm, 1)

            def prepare_ab(k, dst):
                pe.wait_ge(ab_staged, 16 * 4 * (k // 2 + 1))
                at = k % 2 * HD
                for h in range(HH):
                    last = nc.tensor.matmul(dst[:, h * D:(h + 1) * D], work[at:at + HD, h * D:(h + 1) * D],
                                            work[at:at + HD, WIDE + h * D:WIDE + (h + 1) * D], start=True, stop=True)
                last.then_inc(prep_mm, 1)

            def layer1(f, t, s):
                e, c = s // FC, s % FC
                pe.wait_ge(gelu_done, did((f * PASSES + t) * STEPS + s - 1))
                w_hi, w_lo = (w[:, e, c * P:(c + 1) * P] for w in (w1_hi, w1_lo))
                dst = h_ps[s % 2]
                for w, m, first, end in ((w_hi, xhi, True, False), (w_hi, xlo, False, False), (w_lo, xhi, False, True)):
                    for j in range(2):
                        last = nc.tensor.matmul(dst[:, j * HALF:(j + 1) * HALF], w,
                                                m[:, bass.ds(t * WIDE + j * HALF, HALF)], start=first, stop=end)
                last.then_inc(l1_done, 1)

            def layer2_hi(p, s):
                e, c = s // FC, s % FC
                pe.wait_ge(gelu_done, did(p * STEPS + s + 1))
                if c == 0:
                    pe.wait_ge(one_done, did(p * E + e - 1))
                for n, w in enumerate((w2_hi, w2_lo)):
                    for j in range(2):
                        last = nc.tensor.matmul(y_ps[e % 2][:, j * HALF:(j + 1) * HALF], w[:, e, c * D:(c + 1) * D],
                                                ring_hi[:, s % 2, j * HALF:(j + 1) * HALF],
                                                start=c == 0 and n == 0, stop=False)
                last.then_inc(hi_used, 1)

            def layer2_lo(p, s):
                e, c = s // FC, s % FC
                pe.wait_ge(lo_done, did(p * STEPS + s + 1))
                for j in range(2):
                    last = nc.tensor.matmul(y_ps[e % 2][:, j * HALF:(j + 1) * HALF], w2_hi[:, e, c * D:(c + 1) * D],
                                            ring_lo[:, s % 2, j * HALF:(j + 1) * HALF], start=False, stop=c == FC - 1)
                last.then_inc(l2_done, 1)

            def transpose_comb(dst):
                nc.tensor.transpose(dst[0:E * WT, 0:P], comb_next[:].rearrange("p e t -> p (e t)"), ident[:]) \
                    .then_inc(combT_mm, 1)

            def transpose_sum(p, dst):
                pe.wait_ge(acc_done, did((p + 1) * (E - 1)))
                for i in range(WT):
                    last = nc.tensor.transpose(dst[:, i * P:(i + 1) * P], y_acc[:, i * P:(i + 1) * P], ident[:])
                last.then_inc(accT_done, 1)

            def rest_of_pass(f, t, prepare):
                p = f * PASSES + t
                ab = f == 0 and not prepare
                n_ln = LN_PASS[f] + t + 1
                for s in range(AHEAD, STEPS):
                    e, spare = s // FC, y_ps[(s // FC + 1) % 2]
                    busy = (STEP_T,) + STEP_R + (STEP_COMB,) if prepare else AB_STEP + (SEQ_T,) if ab else ()
                    if s in busy:
                        pe.wait_ge(one_done, did(p * E + e))
                    if prepare and s == STEP_COMB:
                        pe.wait_ge(comb_ready, did(p + 2))
                    if s < STEPS - 1:
                        layer1(f, t, s + 1)
                    elif prepare:
                        layer1(f, t + 1, 0)
                    if s in busy:
                        if ab and s == SEQ_T:
                            transpose_x(LN_SEQ, spare, QT)
                        elif ab:
                            prepare_ab(AB_STEP.index(s), spare)
                        elif s == STEP_T:
                            transpose_x(n_ln, spare, WT)
                        elif s in STEP_R:
                            half = STEP_R.index(s)
                            pe.wait_ge(xlo_done, did(n_ln + 1))
                            route(half, spare)
                        else:
                            transpose_comb(spare)
                    if prepare and s == (STEP_T // FC + 1) * FC:
                        pe.wait_ge(xlo_done, did(n_ln + 1))
                    for half in range(2):
                        if prepare and s == (STEP_R[half] // FC + 1) * FC:
                            pe.wait_ge(r_done, did(2 * (p + 1) + half + 1))
                    if ab and s - 2 in AB_STEP:
                        pe.wait_ge(w_done, did(len(DVE_CHUNKS) + AB_STEP.index(s - 2) + 1))
                    if ab and s - 2 == SEQ_T:
                        pe.wait_ge(xlo_done, did(LN_SEQ + 1))
                    layer2_hi(p, s)
                    layer2_lo(p, s - 1)
                if not prepare:
                    layer2_lo(p, STEPS - 1)
                    return
                for s in range(AHEAD):
                    layer1(f, t + 1, s + 1)
                    if s == 0:
                        pe.wait_ge(combT_done, did(p + 2))
                    if s == STEP_SUM:
                        transpose_sum(p, y_ps[1])
                    if s == FC:
                        pe.wait_ge(xup_done, did(p + 1))
                    layer2_hi(p + 1, s)
                    if s > 0:
                        layer2_lo(p + 1, s - 1)
                    else:
                        layer2_lo(p, STEPS - 1)

            def latent(dst, b, token_major):
                if not token_major:
                    nc.tensor.matmul(dst, w_down_sb[:], xT[:, 0:SEQ], start=True, stop=True).then_inc(lat_mm, 1)
                else:
                    for i in range(QT):
                        last = nc.tensor.matmul(dst[:, i * P:(i + 1) * P], xT[:, i * P:(i + 1) * P], w_down_sb[:],
                                                start=True, stop=True)
                    last.then_inc(lat_mm, 1)

            def attention_slot(b0, i, live, prepare):
                def unit(u):
                    return b0 * HEADS + u, u % HEADS, b0 + u // HEADS
                if live(i + 3):
                    n, h, b = unit(i + 3)
                    pe.wait_ge(qev_done, did(n + 1))
                    pe.wait_ge(exp_done, did(n - 1))
                    if h == 0:
                        pe.wait_ge(lat_done, did(2 * b + 1))
                    dst, q = s_bank[(i + 3) % 2], q_ring[(i + 3) % 2]
                    nc.tensor.matmul(dst[:, P:PC], q[:, P:SEQ], lat_T[:, bass.ds(b * SEQ, SEQ)], start=True, stop=False,
                                     skip_group_check=True)
                    nc.tensor.matmul(dst[:, 0:P], q[:, 0:P], lat_T[:, bass.ds(b * SEQ, P)], start=False, stop=False,
                                     skip_group_check=True)
                    nc.tensor.matmul(dst[:, 0:P], ident_bf[:], causal_bf[:], start=False, stop=False,
                                     skip_group_check=True)
                    nc.tensor.matmul(dst[:, 2 * P:PC], ident_bf[:], causal_bf[:], start=False, stop=True,
                                     skip_group_check=True).then_inc(s_done, 1)
                if live(i + 4):
                    n, h, b = unit(i + 4)
                    pe.wait_ge(qev_done, did(n))
                    if h == 0:
                        pe.wait_ge(xlo_done, did(LN_SEQ + b + 1))
                    m_hi, m_lo = (m[:, bass.ds(b * SEQ, SEQ)] for m in (xhi, xlo))
                    nc.tensor.matmul(q_bank[:, 0:SEQ], a_hi[:, h, :], m_hi, start=True, stop=False)
                    nc.tensor.matmul(q_bank[:, 0:SEQ], a_hi[:, h, :], m_lo, start=False, stop=False)
                    nc.tensor.matmul(q_bank[:, 0:SEQ], a_lo[:, h, :], m_hi, start=False, stop=True).then_inc(q_done, 1)
                if live(i + 1):
                    n, h, b = unit(i + 1)
                    pe.wait_ge(pn_done, did(n + 1))
                    pe.wait_ge(pt_done, did(n - 1))
                    for k in range(3):
                        last = nc.tensor.transpose(t_bank[(i + 1) % 2][:, k * P:(k + 1) * P],
                                                   p_ring[(i + 1) % 2][:, k * P:(k + 1) * P], ident[:])
                    last.then_inc(t_done, 1)
                z, beside = z_bank[i % 2][:, 0:SEQ], z_bank[i % 2][:, SEQ:2 * SEQ]
                if live(i):
                    n, h, b = unit(i)
                    pe.wait_ge(pt_done, did(n + 1))
                    pe.wait_ge(zlo_done, did(n - 1))
                if i % HEADS == 2 and live(i - 3):
                    b = unit(i - 3)[2]
                    pe.wait_ge(oev_done, did(b + 1))
                    if not live(i):
                        pe.wait_ge(zlo_done, did(UNITS))
                    for j in range(QT):
                        last = nc.tensor.transpose(beside[:, j * P:(j + 1) * P], o_sb[:, j * P:(j + 1) * P], ident[:])
                    last.then_inc(oT_done, 1)
                job = slot_job(2, b0, i) if prepare else None
                if job:
                    transpose_x(job[0], beside, QT, job[2] * QT)
                if prepare and not last_sequence(b0) and i == 8:
                    pe.wait_ge(xlo_done, did(LN_SEQ + b0 + 2))
                    latent(beside, b0 + 1, False)
                if prepare and not last_sequence(b0) and i == 9:
                    latent(beside, b0 + 1, True)
                if live(i):
                    n, h, b = unit(i)
                    if h == 0:
                        pe.wait_ge(latcur_done, did(b + 1))
                    pt = pt_ring[i % 2]
                    nc.tensor.matmul(z, lat_cur[:, 0, :], pt[:, 0:SEQ], start=True, stop=False)
                    nc.tensor.matmul(z[:, P:SEQ], lat_cur[:, 1, :], pt[:, SEQ:PC], start=False, stop=True) \
                        .then_inc(z_done, 1)
                if live(i - 1):
                    n, h, b = unit(i - 1)
                    pe.wait_ge(zlo_done, did(n + 1))
                    if h == 0:
                        pe.wait_ge(oev_done, did(b))
                    z_hi, z_lo = (r[:, (i - 1) % 2, 0:SEQ] for r in (ring_hi, ring_lo))
                    first, last = h == 0, h == HEADS - 1
                    nc.tensor.matmul(o_bank[:, 0:SEQ], b_hi[:, h, :], z_hi, start=first, stop=False)
                    nc.tensor.matmul(o_bank[:, 0:SEQ], b_hi[:, h, :], z_lo, start=False, stop=False)
                    nc.tensor.matmul(o_bank[:, 0:SEQ], b_lo[:, h, :], z_hi, start=False, stop=last).then_inc(o_done, 1)

            def begin(f):
                n_ln = LN_PASS[f]
                if f == 0:
                    transpose_x(0, y_ps[1], WT)
                    prepare_router()
                    pe.wait_ge(xlo_done, did(1))
                    pe.wait_ge(w_done, did(1))
                else:
                    pe.wait_ge(oev_done, did(BATCH))
                layer1(f, 0, 0)
                if f == 1:
                    pe.wait_ge(exp_done, did(UNITS))
                layer1(f, 0, 1)
                if f == 0:
                    pe.wait_ge(rw_done, did(3))
                else:
                    pe.wait_ge(xres_done, did(BATCH))
                route(0, y_ps[1])
                pe.wait_ge(r_done, did(2 * f * PASSES + 1))
                route(1, y_ps[1])
                for s in range(AHEAD):
                    if 0 < s < AHEAD - 1:
                        layer1(f, 0, s + 1)
                    if s == 0 and f == 0:
                        pe.wait_ge(w_done, did(2))
                    if s == 0 and f == 1:
                        pe.wait_ge(pt_done, did(UNITS))
                    if s == FC:
                        pe.wait_ge(r_done, did(2 * (f * PASSES + 1)))
                    if s == AHEAD - 1:
                        pe.wait_ge(comb_ready, did(f * PASSES + 1))
                        transpose_comb(h_ps[AHEAD % 2])
                        if f == 0:
                            pe.wait_ge(w_done, did(3))
                        pe.wait_ge(combT_done, did(f * PASSES + 1))
                        layer1(f, 0, AHEAD)
                    layer2_hi(f * PASSES, s)
                    if s > 0:
                        layer2_lo(f * PASSES, s - 1)

            begin(0)
            pe.wait_ge(w_done, did(len(DVE_CHUNKS)))
            pe.wait_ge(wp_done, did(len(POOL_CHUNKS)))
            run_passes(pe, rest_of_pass, 0)
            latent(s_bank[0][:, 0:SEQ], 0, False)
            latent(s_bank[1][:, 0:SEQ], 0, True)
            transpose_sum(PASSES - 1, y_ps[0])
            pe.wait_ge(xup_done, did(PASSES))
            run_slots(pe, attention_slot)
            begin(1)
            run_passes(pe, rest_of_pass, 1)
            transpose_sum(2 * PASSES - 1, y_ps[0])

        @block.scalar
        def _(act):
            for own in (xhi_done, gelu_done, exp_done, pt_done, zhi_done, wsplit_hi):
                act.sem_inc(own, CREDIT)
            A = nc.scalar.activation

            def copy_x(n, src, col, cols, at=0):
                act.wait_ge(xt_ready, did(n + 1))
                A(xhi[:, bass.ds(col, cols)], src, ACT.Copy)
                A(xT[:, at:at + cols], src, ACT.Copy).then_inc(xhi_done, 1)

            def split_weights(k):
                act.wait_ge(staged[k], 16)
                A(weight_chunk(k)[0], stage[k], ACT.Copy).then_inc(wsplit_hi, 1)

            def load_ab(weights):
                for j, w in enumerate(weights):
                    for hh in range(2):
                        act.dma_start(work[hh * HD:(hh + 1) * HD, j * WIDE:(j + 1) * WIDE].rearrange("p (h d) -> p h d", d=D),
                                      w[:, hh * HH:(hh + 1) * HH, :]).then_inc(ab_staged, 16)

            def split_ab(k, src):
                act.wait_ge(prep_mm, did(2 + k + 1))
                dst = (a_hi, b_hi)[k // 2][:, (k % 2) * HH:(k % 2 + 1) * HH, :].rearrange("p h d -> p (h d)")
                A(dst, src, ACT.Copy, scale=(HD ** -0.5, 1.0)[k // 2]).then_inc(wsplit_hi, 1)

            def step(p, s):
                e, c = s // FC, s % FC
                n = p * STEPS + s
                act.wait_ge(l1_done, did(n + 1))
                act.wait_ge(lo_done, did(n - 1))
                A(h_ring[:, s % 2, :], h_ps[s % 2][:], ACT.Gelu, bias=b1_sb[:, e, c:c + 1])
                act.wait_ge(hi_used, did(n - 1))
                A(ring_hi[:, s % 2, :], h_ps[s % 2][:], ACT.Gelu, bias=b1_sb[:, e, c:c + 1]).then_inc(gelu_done, 1)

            def rest_of_pass(f, t, prepare):
                p = f * PASSES + t
                ab = f == 0 and not prepare
                for s in range(AHEAD, STEPS):
                    step(p, s)
                    spare = y_ps[(s // FC + 1) % 2]
                    if prepare and s == STEP_T:
                        copy_x(LN_PASS[f] + t + 1, spare[:], (t + 1) * WIDE, WIDE)
                    if ab and s in AB_STEP:
                        split_ab(AB_STEP.index(s), spare[:])
                        if s == AB_STEP[1]:
                            load_ab((wuv_t, w_out))
                    if ab and s == SEQ_T:
                        copy_x(LN_SEQ, spare[:, 0:SEQ], 0, SEQ)
                if prepare:
                    for s in range(AHEAD):
                        step(p + 1, s)

            def attention_slot(b0, i, live, prepare):
                def unit(u):
                    return b0 * HEADS + u
                if live(i - 1):
                    n, k = unit(i - 1), (i - 1) % 2
                    act.wait_ge(z_done, did(n + 1))
                    act.wait_ge(o_done, did(n - 1))
                    A(ring_hi[:, k, 0:SEQ], z_bank[k][:, 0:SEQ], ACT.Copy).then_inc(zhi_done, 1)
                job = slot_job(3, b0, i) if prepare else None
                if job:
                    copy_x(job[0], z_bank[(i - 1) % 2][:, SEQ:2 * SEQ], job[1] * SEQ, SEQ, job[2] * SEQ)
                if live(i + 1):
                    n, k = unit(i + 1), (i + 1) % 2
                    act.wait_ge(t_done, did(n + 1))
                    act.wait_ge(z_done, did(n - 1))
                    A(pt_ring[k], t_bank[k][:, 0:PC], ACT.Copy).then_inc(pt_done, 1)
                if live(i + 3):
                    n, k = unit(i + 3), (i + 3) % 2
                    act.wait_ge(max_done, did(n + 1))
                    act.wait_ge(t_done, did(n - 1))
                    A(p_ring[k][:, 0:P], s_bank[k][:, 0:P], ACT.Exp, bias=neg_max[:, k, 0:1], accum_out=row_sum[:, k, 0:1])
                    A(p_ring[k][:, P:PC], s_bank[k][:, P:PC], ACT.Exp, bias=neg_max[:, k, 1:2],
                      accum_out=row_sum[:, k, 1:2]).then_inc(exp_done, 1)

            copy_x(0, y_ps[1][:], 0, WIDE)
            act.wait_ge(small_loaded, SMALL)
            for k in range(2):
                split_weights(k)
            for s in range(AHEAD):
                step(0, s)
                if 2 + s < W_CHUNKS:
                    split_weights(2 + s)
            act.wait_ge(w_done, did(len(DVE_CHUNKS)))
            act.wait_ge(wp_done, did(len(POOL_CHUNKS)))
            load_ab((wq_t, wuk_t))
            run_passes(act, rest_of_pass, 0)
            run_slots(act, attention_slot)
            for s in range(AHEAD):
                step(PASSES, s)
            run_passes(act, rest_of_pass, 1)

        @block.vector
        def _(dve):
            for own in (dve_chain, ln_in, norm_in, arg_in, norm_done, xlo_done, w_done, rw_done, r_done, lat_done,
                        comb_ready, combT_done, lo_done, one_done, xup_done, qev_done,
                        max_done, rec_done, pn_done, zlo_done, latcur_done, oev_done, xres_done):
                dve.sem_inc(own, CREDIT)
            V = nc.vector
            PASS_LINKS, SEQ_LINKS = 34, 2
            links = [0, 0]
            before_moe, before_attention = [0, 0], [0]

            def link(instruction):
                links[1] = links[1] + 1
                instruction.then_inc(dve_chain, 1)
                dve.wait_ge(dve_chain, did(links[0] + links[1]))

            def ln_stats(tile, tiles):
                for i in range(tiles):
                    last = V.bn_stats(stats[:, i, :], x_flat[:, bass.ds((tile + i) * D, D)])
                link(last)
                V.tensor_copy(after_wait[:], stats[:, 0, 0:1])
                for i in range(tiles):
                    last = V.bn_aggr(mean_var[:, i, :], stats[:, i, :])
                link(last)
                V.tensor_scalar(var_eps[:, 0:tiles], mean_var[:, 0:tiles, 1], LN_EPS, None, ALU.add).then_inc(ln_in, 1)

            def ln_apply(n, tile, tiles, at=0):
                dve.wait_ge(ln_root, did(n + 1))
                for i in range(tiles):
                    last = V.tensor_scalar(xn[:, at + i, :], x_flat[:, bass.ds((tile + i) * D, D)], mean_var[:, i, 0:1],
                                           rstd[:, i:i + 1], ALU.subtract, ALU.mult)
                last.then_inc(norm_done, 1)

            def x_lo(n, src, col, cols):
                dve.wait_ge(xhi_done, did(n + 1))
                V.tensor_tensor(xlo[:, bass.ds(col, cols)], src, xhi[:, bass.ds(col, cols)].bitcast(F32), ALU.subtract) \
                    .then_inc(xlo_done, 1)

            def per_token(v):
                return v.unsqueeze(2).broadcast_to([P, WT, E])

            def per_expert(v):
                return v.unsqueeze(1).broadcast_to([P, WT, E])

            def route_evacuate(p, half, src):
                dve.wait_ge(route_mm, did(2 * p + half + 1))
                got = src[:].rearrange("p (b c) -> p b c", b=2)[:, :, 0:2 * R_COLS] \
                    .rearrange("p b (t c) -> p b t c", t=2)
                n = WT // 2
                r = xn[:, half * n:(half + 1) * n, :].rearrange("p (b t) d -> p b t d", b=2)
                d = r_dot[:, half * n:(half + 1) * n, :].rearrange("p (b t) e -> p b t e", b=2)
                for b in range(2):
                    V.tensor_tensor(r[:, b, :, :], got[:, b, :, 0:D], router_b[:, 0:D].unsqueeze(1).broadcast_to([P, 2, D]), ALU.add)
                    last = V.tensor_tensor(d[:, b, :, :], got[:, b, :, D:R_COLS],
                                           router_b[:, D:R_COLS].unsqueeze(1).broadcast_to([P, 2, E]), ALU.add)
                last.then_inc(r_done, 1)

            n2, root, scale, xn2, one_m, m_1, k_1, n2_clip = (tok_s[:, k, :] for k in range(8))

            def route_norms(p):
                dve.wait_ge(r_done, did(2 * (p + 1)))
                link(V.tensor_tensor(xn, xn, xn, ALU.mult))
                link(V.tensor_reduce(n2, xn, AX.X, ALU.add))
                V.tensor_scalar(n2_clip, n2, BALL_EPS * BALL_EPS, None, ALU.max).then_inc(norm_in, 1)

            def route_args(p):
                dve.wait_ge(norm_root, did(1 + p + 1))
                link(V.tensor_scalar(scale, root, MAX_NORM, 1.0, ALU.mult, ALU.min))
                V.tensor_tensor(dot, r_dot[:], per_token(scale), ALU.mult)
                link(V.tensor_tensor(xn2, scale, scale, ALU.mult))
                link(V.tensor_tensor(xn2, xn2, n2, ALU.mult))
                link(V.tensor_scalar(xn2, xn2, MAX_SQ, None, ALU.min))
                V.scalar_tensor_tensor(arg, dot, -2.0, per_expert(cn2[:, 0, :]), ALU.mult, ALU.add)
                link(V.tensor_scalar(one_m, xn2, -1.0, 1.0, ALU.mult, ALU.add))
                V.tensor_tensor(arg, arg, per_token(xn2), ALU.add)
                link(V.tensor_tensor(den, per_expert(cn2[:, 1, :]), per_token(one_m), ALU.mult))
                link(V.tensor_scalar(den, den, BALL_EPS, None, ALU.add))
                link(V.reciprocal(den, den))
                link(V.scalar_tensor_tensor(arg, arg, 0.0, den, ALU.max, ALU.mult))
                link(V.tensor_scalar(arg, arg, 2.0, 1.0, ALU.mult, ALU.add))
                link(V.tensor_scalar(arg, arg, 1.0 + BALL_EPS, None, ALU.max))

            def nearest(sel, values, least):
                link(V.tensor_reduce(least, values, AX.X, ALU.min))
                link(V.tensor_tensor(tmp, values, per_token(least), ALU.is_equal))
                link(V.tensor_tensor(tmp, tmp, per_expert(rank[:]), ALU.mult))
                link(V.tensor_reduce(k_1, tmp, AX.X, ALU.max))
                link(V.tensor_tensor(sel, tmp, per_token(k_1), ALU.is_equal))

            def route_second():
                link(V.scalar_tensor_tensor(den, sel1, 1e30, arg, ALU.mult, ALU.add))
                nearest(sel2, den, tok_2[:, 0, 1, :])
                link(V.tensor_scalar(tok_2[:, 1, :, :], tok_2[:, 0, :, :], 1.0, None, ALU.add))
                V.scalar_tensor_tensor(tok_2[:, 1, :, :], tok_2[:, 0, :, :], -1.0, tok_2[:, 1, :, :], ALU.add, ALU.mult) \
                    .then_inc(arg_in, 1)

            def route_weights(p):
                dve.wait_ge(arg_root, did(p + 1))
                link(V.tensor_tensor(tok_2[:, 0, :, :], tok_2[:, 0, :, :], tok_2[:, 2, :, :], ALU.add))
                link(V.reciprocal(m_1, tok_2[:, 0, 1, :]))
                link(V.tensor_tensor(m_1, m_1, tok_2[:, 0, 0, :], ALU.mult))
                link(V.tensor_scalar(k_1, m_1, 1.0, None, ALU.add))
                link(V.reciprocal(k_1, k_1))
                link(V.tensor_tensor(m_1, m_1, k_1, ALU.mult))
                V.tensor_tensor(sel1, sel1, per_token(k_1), ALU.mult)
                link(V.tensor_tensor(sel2, sel2, per_token(m_1), ALU.mult))
                V.tensor_tensor(comb_next[:].rearrange("p e t -> p t e"), sel1, sel2, ALU.add).then_inc(comb_ready, 1)

            def prepare_router():
                dve.wait_ge(small_loaded, SMALL)
                sq = lat_next[0:E, 0, :]
                link(V.tensor_tensor(sq, cent, cent, ALU.mult))
                link(V.tensor_reduce(cent_s[:, 2:3], sq, AX.X, ALU.add))
                V.tensor_scalar(cent_s[:, 0:1], cent_s[:, 2:3], BALL_EPS * BALL_EPS, None, ALU.max).then_inc(norm_in, 1)
                dve.wait_ge(norm_root, did(1))
                link(V.tensor_scalar(cent_s[:, 3:4], cent_s[:, 1:2], MAX_NORM, 1.0, ALU.mult, ALU.min))
                V.tensor_scalar(cent, cent, cent_s[:, 3:4], None, ALU.mult).then_inc(rw_done, 1)
                dve.wait_ge(prep_mm, did(1))
                link(V.tensor_copy(cent_t[:], bank[5][:, 0:E]))
                V.tensor_tensor(cent_sq[:], cent_t[:], cent_t[:], ALU.mult).then_inc(rw_done, 1)
                dve.wait_ge(prep_mm, did(2))
                link(V.tensor_scalar(cn2[:, 0, :], bank[4][:, 0:E], MAX_SQ, None, ALU.min))
                V.tensor_scalar(cn2[:, 1, :], cn2[:, 0, :], -1.0, 1.0, ALU.mult, ALU.add)
                V.tensor_copy(router_w[:, D:R_COLS], bank[4][:, P:P + E])
                V.tensor_copy(router_b[:], bank[4][:, 2 * P:2 * P + R_COLS]).then_inc(rw_done, 1)

            def split_weights(k):
                dve.wait_ge(wsplit_hi, did(k + 1))
                hi, lo = weight_chunk(k)
                V.tensor_tensor(lo, stage[k], hi.bitcast(F32), ALU.subtract).then_inc(w_done, 1)

            def split_ab(k, src):
                dve.wait_ge(wsplit_hi, did(W_CHUNKS + k + 1))
                hi, lo = (w[:, (k % 2) * HH:(k % 2 + 1) * HH, :].rearrange("p h d -> p (h d)")
                          for w in ((a_hi, a_lo), (b_hi, b_lo))[k // 2])
                V.scalar_tensor_tensor(lo, src, (HD ** -0.5, 1.0)[k // 2], hi.bitcast(F32),
                                       ALU.mult, ALU.subtract).then_inc(w_done, 1)

            def lo_of_step(p, s):
                n = p * STEPS + s
                dve.wait_ge(gelu_done, did(n + 1))
                dve.wait_ge(l2_done, did(n - 1))
                V.tensor_tensor(ring_lo[:, s % 2, :], h_ring[:, s % 2, :], ring_hi[:, s % 2, :].bitcast(F32),
                                ALU.subtract).then_inc(lo_done, 1)

            def fold(p, e):
                dve.wait_ge(l2_done, did(p * STEPS + (e + 1) * FC))
                dve.wait_ge(comb_loaded[e % 2], 16 * (p * (E // 2) + e // 2 + 1) + CREDIT)
                if e > 1:
                    dve.wait_ge(acc_done, did(p * (E - 1) + e - 1))
                V.scalar_tensor_tensor(y_acc if e == 0 else y_one, y_ps[e % 2][:], b2_sb[:, e:e + 1], comb_b[:, e % 2, :],
                                       ALU.add, ALU.mult).then_inc(one_done, 1)

            def comb_evacuate(p, src):
                dve.wait_ge(combT_mm, did(p + 1))
                V.tensor_copy(comb_T, src[0:E * WT, 0:P]).then_inc(combT_done, 1)

            def update_x(p, t, src):
                dve.wait_ge(accT_done, did(p + 1))
                here = x_flat[:, bass.ds(t * WIDE, WIDE)]
                V.scalar_tensor_tensor(here, src, 0.5, here, ALU.mult, ALU.add).then_inc(xup_done, 1)

            def rest_of_pass(f, t, prepare):
                p = f * PASSES + t
                ab = f == 0 and not prepare
                n_ln = LN_PASS[f] + t + 1
                links[:] = before_moe[f] + t * PASS_LINKS, 0
                for s in range(AHEAD, STEPS):
                    lo_of_step(p, s)
                    spare = y_ps[(s // FC + 1) % 2]
                    if s % FC == 0:
                        fold(p, s // FC - 1)
                    if prepare:
                        if s == STEP_STATS:
                            if f == 0:
                                dve.wait_ge(x_loaded, 16)
                            ln_stats((t + 1) * WT, WT)
                        if s == STEP_NORM:
                            ln_apply(n_ln, (t + 1) * WT, WT)
                        if s == STEP_XLO:
                            x_lo(n_ln, spare[:], (t + 1) * WIDE, WIDE)
                        if s in STEP_R:
                            route_evacuate(p + 1, STEP_R.index(s), spare)
                        if s == STEP_SQ:
                            route_norms(p + 1)
                        if s == STEP_ARGS:
                            route_args(p + 1)
                        if s == STEP_NEAR:
                            nearest(sel1, arg, tok_2[:, 0, 0, :])
                        if s == STEP_SECOND:
                            route_second()
                        if s == STEP_WEIGHTS:
                            route_weights(p + 1)
                        if s == STEP_COMB:
                            dve.wait_ge(comb_stored, 16 * (p + 1))
                            comb_evacuate(p + 1, spare)
                    if ab:
                        if s - 1 in AB_STEP:
                            split_ab(AB_STEP.index(s - 1), spare[:])
                        if s == SEQ_STATS:
                            ln_stats(0, QT)
                        if s == SEQ_NORM:
                            ln_apply(LN_SEQ, 0, QT)
                        if s == SEQ_XLO:
                            x_lo(LN_SEQ, spare[:, 0:SEQ], 0, SEQ)
                assert links[1] == (PASS_LINKS if prepare else SEQ_LINKS if ab else 0), links
                if prepare:
                    for s in range(AHEAD):
                        lo_of_step(p + 1, s)
                        if s == 0:
                            fold(p, E - 1)
                        if s == STEP_UPDATE:
                            update_x(p, t, y_ps[1][:])
                        if s == FC:
                            fold(p + 1, 0)
                else:
                    if ab:
                        latent_evacuate(0, s_bank[0][:, 0:SEQ], 0)
                    fold(p, E - 1)
                    if ab:
                        latent_evacuate(0, s_bank[1][:, 0:SEQ], 1)
                    update_x(p, t, y_ps[0][:])
                    dve.wait_ge(xup_done, did(p + 1))

            def begin(f):
                p = f * PASSES
                if f == 0:
                    dve.wait_ge(x_loaded0, 16)
                    ln_stats(0, WT)
                    ln_apply(0, 0, WT)
                    prepare_router()
                    x_lo(0, y_ps[1][:], 0, WIDE)
                    split_weights(0)
                    split_weights(1)
                for half in range(2):
                    route_evacuate(p, half, y_ps[1])
                route_norms(p)
                lo_of_step(p, 0)
                route_args(p)
                lo_of_step(p, 1)
                nearest(sel1, arg, tok_2[:, 0, 0, :])
                if f == 0:
                    split_weights(2)
                lo_of_step(p, 2)
                route_second()
                lo_of_step(p, 3)
                if f == 0:
                    split_weights(4)
                lo_of_step(p, 4)
                route_weights(p)
                lo_of_step(p, 5)
                if f == 0:
                    split_weights(6)
                lo_of_step(p, 6)
                if f == 1:
                    dve.wait_ge(comb_stored, 16 * p)
                comb_evacuate(p, h_ps[AHEAD % 2])
                lo_of_step(p, 7)
                if f == 0:
                    dve.wait_ge(wp_done, did(len(POOL_CHUNKS)))
                fold(p, 0)

            def latent_evacuate(b, src, token_major):
                dve.wait_ge(lat_mm, did(2 * b + 1 + token_major))
                dst = lat_next[:].rearrange("p q d -> p (q d)") if token_major else lat_T[:, bass.ds(b * SEQ, SEQ)]
                V.tensor_copy(dst, src).then_inc(lat_done, 1)

            def attention_slot(b0, i, live, prepare):
                def unit(u):
                    return b0 * HEADS + u, b0 + u // HEADS
                if i % HEADS == 0 and live(i):
                    n, b = unit(i)
                    dve.wait_ge(lat_done, did(2 * b + 2))
                    dve.wait_ge(z_done, did(n))
                    V.tensor_copy(lat_cur[:], lat_next[:]).then_inc(latcur_done, 1)
                if live(i + 2):
                    n, k = unit(i + 2)[0], (i + 2) % 2
                    dve.wait_ge(exp_done, did(n + 1))
                    V.reciprocal(row_rec[:, k, :], row_sum[:, k, :]).then_inc(rec_done, 1)
                    dve.wait_ge(rec_done, did(n + 1))
                    for j, cols in ((0, slice(0, P)), (1, slice(P, PC))):
                        last = V.tensor_scalar(p_ring[k][:, cols], p_ring[k][:, cols], row_rec[:, k, j:j + 1], None, ALU.mult)
                    last.then_inc(pn_done, 1)
                if live(i - 1):
                    n, k = unit(i - 1)[0], (i - 1) % 2
                    dve.wait_ge(zhi_done, did(n + 1))
                beside = z_bank[(i - 1) % 2][:, SEQ:2 * SEQ]
                if i % HEADS == 3 and live(i - 4):
                    b = unit(i - 4)[1]
                    dve.wait_ge(oT_done, did(b + 1))
                    here = x_flat[:, bass.ds(b * SEQ, SEQ)]
                    V.tensor_tensor(here, here, beside, ALU.add).then_inc(xres_done, 1)
                job = slot_job(3, b0, i) if prepare else None
                if job:
                    x_lo(job[0], beside, job[1] * SEQ, SEQ)
                if prepare and not last_sequence(b0) and i in (9, 10):
                    latent_evacuate(b0 + 1, beside, i - 9)
                if live(i - 1):
                    n, k = unit(i - 1)[0], (i - 1) % 2
                    dve.wait_ge(o_done, did(n - 1))
                    V.tensor_tensor(ring_lo[:, k, 0:SEQ], z_bank[k][:, 0:SEQ], ring_hi[:, k, 0:SEQ].bitcast(F32),
                                    ALU.subtract).then_inc(zlo_done, 1)
                if i % HEADS == 1 and live(i - 2):
                    n, b = unit(i - 2)
                    dve.wait_ge(o_done, did(n + 1))
                    dve.wait_ge(oT_done, did(b))
                    V.tensor_copy(o_sb[:], o_bank[:, 0:SEQ]).then_inc(oev_done, 1)
                if live(i + 3):
                    n, k = unit(i + 3)[0], (i + 3) % 2
                    dve.wait_ge(s_done, did(n + 1))
                    dve.wait_ge(exp_done, did(n - 1))
                    V.tensor_reduce(neg_max[:, k, 0:1], s_bank[k][:, 0:P], AX.X, ALU.max, negate=True)
                    V.tensor_reduce(neg_max[:, k, 1:2], s_bank[k][:, P:PC], AX.X, ALU.max, negate=True) \
                        .then_inc(max_done, 1)
                if live(i + 4):
                    n, k = unit(i + 4)[0], i % 2
                    dve.wait_ge(q_done, did(n + 1))
                    dve.wait_ge(s_done, did(n - 1))
                    V.tensor_copy(q_ring[k], q_bank[:, 0:SEQ]).then_inc(qev_done, 1)
                job = slot_job(0, b0, i) if prepare else None
                if job:
                    links[:] = before_attention[0] + (job[0] - LN_SEQ - 1) * SEQ_LINKS, 0
                    ln_stats(job[1] * QT, QT)
                job = slot_job(1, b0, i) if prepare else None
                if job:
                    ln_apply(job[0], job[1] * QT, QT, job[2] * QT)

            begin(0)
            before_moe[0] = sum(links)
            run_passes(dve, rest_of_pass, 0)
            before_attention[0] = sum(links)
            run_slots(dve, attention_slot)
            begin(1)
            before_moe[1] = sum(links)
            run_passes(dve, rest_of_pass, 1)
    return nc


_OUT = (16, 256, 128)


def kernel(**inputs):
    import numpy as _np
    import concourse.bacc as _bacc
    from concourse import mybir as _mybir
    from concourse.bass_utils import run_bass_kernel_spmd as _run

    a = {k: _np.asarray(v) for k, v in inputs.items()}
    C = a["L0_attn_x"].shape[-1]
    E, _, F = a["L0_ffn_W1"].shape
    HD = 64
    HEADS = a["L0_attn_w_q"].shape[1] // HD
    up = a["L0_attn_w_kv_up"]
    cut = HEADS * HD
    laid = {
        "x": a["L0_attn_x"],
        "w_down": a["L0_attn_w_kv_down"],
        "wq_t": a["L0_attn_w_q"].T.reshape(HEADS, HD, C).transpose(1, 0, 2),
        "wuk_t": up[:, :cut].T.reshape(HEADS, HD, C).transpose(1, 0, 2),
        "wuv_t": up[:, cut:].T.reshape(HEADS, HD, C).transpose(1, 0, 2),
        "w_out": a["L0_attn_w_out"].reshape(HEADS, HD, C).transpose(1, 0, 2),
        "centroids": a["L0_ffn_centroids"],
        "wp_t": a["L0_ffn_Wp"].T,
        "wp": a["L0_ffn_Wp"],
        "bp": a["L0_ffn_bp"].reshape(C, 1),
        "w1": a["L0_ffn_W1"].transpose(1, 0, 2),
        "b1": a["L0_ffn_b1"].reshape(E, F // 128, 128).transpose(2, 0, 1),
        "w2": a["L0_ffn_W2"].reshape(E, F // 128, 128, C).transpose(2, 0, 1, 3).reshape(128, E, F // 128 * C),
        "b2": a["L0_ffn_b2"].T,
    }
    nc = _bacc.Bacc("TRN2", target_bir_lowering=False, num_devices=1)
    arrays, args = {}, []
    for name, v in laid.items():
        v = _np.ascontiguousarray(v)
        arrays[f"in_{name}"] = v
        args.append(nc.dram_tensor(f"in_{name}", v.shape, _mybir.dt.from_np(v.dtype), kind="ExternalInput").ap())
    out = nc.dram_tensor("out", _OUT, _mybir.dt.float32, kind="ExternalOutput").ap()
    macaron_block(nc, *args, out)
    r = _run(nc, [arrays], core_ids=[0])
    return r.results[0]["out"]
```

```python
import concourse.bass as bass
from concourse import mybir
from contextlib import ExitStack

F32 = mybir.dt.float32
F32R = mybir.dt.float32r
BF16 = mybir.dt.bfloat16
ALU = mybir.AluOpType
ACT = mybir.ActivationFunctionType
AX = mybir.AxisListType

P = 128
CREDIT = 2


def macaron_block(nc, x, w_down, wq_t, wuk_t, wuv_t, w_out, centroids, wp_t, wp, bp, w1, b1, w2, b2, out):
    BATCH, SEQ, D = x.shape
    HD, HEADS, _ = wq_t.shape
    E, FC = w1.shape[1], w1.shape[2] // P
    TOKENS = BATCH * SEQ
    TILES = TOKENS // P
    QT = SEQ // P
    WT = 8
    WIDE = WT * P
    PASSES = TOKENS // WIDE
    STEPS = E * FC
    UNITS = BATCH * HEADS
    LN_EPS, BALL_EPS, MAX_NORM, MAX_SQ = 1e-5, 1e-7, 0.95, 0.99
    HALF = 512
    R_COLS = D + E
    PC = QT * (QT + 1) // 2 * P
    assert QT == 2 and WIDE == 2 * HALF and FC == 4

    ctx = ExitStack()
    with ctx:
        def sb(name, shape, dt=F32):
            return ctx.enter_context(nc.sbuf_tensor(name, shape, dt))

        def sem(name):
            return ctx.enter_context(nc.semaphore(name))

        x_tok = sb("x_tok", [P, TILES, D])
        x_flat = x_tok[:].rearrange("p t d -> p (t d)")
        x_lat_hi = sb("x_lat_hi", [P, SEQ + TOKENS], F32R)
        x_lat_lo = sb("x_lat_lo", [P, SEQ + TOKENS], F32R)
        xhi, xlo = x_lat_hi[:, SEQ:], x_lat_lo[:, SEQ:]
        w1_hi = sb("w1_hi", [P, E, FC * P], F32R)
        w1_lo = sb("w1_lo", [P, E, FC * P], F32R)
        w2_hi = sb("w2_hi", [P, E, FC * D], F32R)
        w2_lo = sb("w2_lo", [P, E, FC * D], F32R)
        a_hi = sb("a_hi", [P, HEADS, D], F32R)
        a_lo = sb("a_lo", [P, HEADS, D], F32R)
        b_hi = sb("b_hi", [P, HEADS, D], F32R)
        b_lo = sb("b_lo", [P, HEADS, D], F32R)
        ring_hi = sb("ring_hi", [P, 2, WIDE], F32R)
        ring_lo = sb("ring_lo", [P, 2, WIDE], F32R)
        big = sb("big", [P, 8 * WIDE])
        work = sb("work", [P, 2 * WIDE])
        ident = sb("ident", [P, P])
        ident_bf = sb("ident_bf", [P, P], BF16)
        causal_bf = sb("causal_bf", [P, P], BF16)
        ones = sb("ones", [P, 1])
        powers = sb("powers", [P, 2])
        comb_next = sb("comb_next", [P, E, WT])
        comb_dram = nc.dram_tensor("comb_dram", (E * WT, P), F32).ap()
        stats = sb("stats", [P, WT, 6])
        after_wait = sb("after_wait", [P, 1])
        mean_var = sb("mean_var", [P, WT, 2])
        var_eps = sb("var_eps", [P, WT])
        rstd = sb("rstd", [P, WT])
        tok_s = sb("tok_s", [P, 8, WT])
        tok_2 = sb("tok_2", [P, 3, 2, WT])
        router_w = sb("router_w", [P, R_COLS])
        router_b = sb("router_b", [P, R_COLS])
        cent_s = sb("cent_s", [E, 4])
        cent_t = sb("cent_t", [P, E])
        cent_sq = sb("cent_sq", [P, E])
        cn2 = sb("cn2", [P, 2, E])
        rank = sb("rank", [P, E])
        bp_col = sb("bp_col", [P, 1])
        b1_sb = sb("b1_sb", [P, E, FC])
        b2_sb = sb("b2_sb", [P, E])
        w_down_sb = sb("w_down_sb", [P, D])
        lat_next = sb("lat_next", [P, QT, P])
        neg_max = sb("neg_max", [P, 2, QT])
        row_sum = sb("row_sum", [P, 2, QT])
        row_rec = sb("row_rec", [P, 2, QT])

        def part(k, n=1):
            return big[:, k * WIDE:(k + n) * WIDE]
        h_ring = part(0, 2).rearrange("p (r n) -> p r n", r=2)
        y_acc, y_one = part(2), part(3)
        comb_b = part(4, 2).rearrange("p (r n) -> p r n", r=2)
        lat_T = part(0, 2)
        xn = part(6).rearrange("p (t d) -> p t d", d=D)
        xT = part(7)
        TE = WT * E
        dot, arg, den, sel1, sel2, tmp = (xT[:, k * TE:(k + 1) * TE].rearrange("p (t e) -> p t e", e=E)
                                          for k in range(6))
        comb_T = lat_next[0:E * WT, 1, :]
        r_dot = lat_next[:, 0, 0:WT * E].rearrange("p (t e) -> p t e", e=E)
        wp_t_sb = part(1)[:, 0:D]
        cent = part(1)[0:E, D:2 * D]
        o_sb = part(4)[:, 0:SEQ]
        stage = [work[:, 0:WIDE], work[:, WIDE:2 * WIDE]] + [part(k) for k in (2, 3, 4, 5)]
        stage += stage[0:2]
        q_ring = [work[:, k * P:(k + 1) * P] for k in range(2)]
        at = 2 * P
        p_ring = [work[:, at + k * PC:at + (k + 1) * PC] for k in range(2)]
        at += 2 * PC
        pt_ring = [work[:, at + k * P:at + (k + 1) * P] for k in range(2)]
        at += 2 * P
        lat_cur = work[:, at:at + P]
        at += P
        assert at <= 2 * WIDE
        rings = (ring_hi, ring_lo)
        z_split, q_split, pt_split = ([[w[:, k, a:a + n] for w in rings] for k in range(2)]
                                      for a, n in ((0, SEQ), (SEQ, P), (SEQ + P, SEQ)))
        at = 2 * SEQ + P
        lat_0_split = [w[:, 0, at:at + SEQ] for w in rings]
        lat_cur_split = [w[:, 0, at + SEQ:at + SEQ + P] for w in rings]
        def lat_T_split(b):
            if isinstance(b, int) and b == 0:
                return lat_0_split
            return [w[:, bass.ds((b - 1) * SEQ, SEQ)] for w in (x_lat_hi, x_lat_lo)]

        pair = [ctx.enter_context(nc.psum_tensor(f"pair{k}", [P, 2 * HALF], F32)) for k in range(4)]
        h_ps = pair[0:2]
        y_ps = pair[2:4]
        bank = [pair[k // 2][:, (k % 2) * HALF:(k % 2 + 1) * HALF] for k in range(8)]
        q_bank, o_bank = bank[0], bank[1]
        s_bank, t_bank, z_bank = bank[2:4], bank[4:6], bank[6:8]

        small_loaded, x_loaded0, x_loaded, stored = sem("small_loaded"), sem("x_loaded0"), sem("x_loaded"), sem("stored")
        comb_stored = sem("comb_stored")
        comb_loaded = [sem(f"comb_loaded{k}") for k in range(2)]
        ab_staged = sem("ab_staged")
        staged = [sem(f"staged{k}") for k in range(8)]
        consts_ready = sem("consts_ready")
        ln_root, norm_root, arg_root = sem("ln_root"), sem("norm_root"), sem("arg_root")
        wp_done = sem("wp_done")
        pn_done = sem("pn_done")
        acc_done = sem("acc_done")
        xt_ready = sem("xt_ready")
        prep_mm = sem("prep_mm")
        route_mm = sem("route_mm")
        lat_mm = sem("lat_mm")
        l1_done = sem("l1_done")
        hi_used = sem("hi_used")
        l2_done = sem("l2_done")
        combT_mm = sem("combT_mm")
        accT_done = sem("accT_done")
        q_done = sem("q_done")
        s_done = sem("s_done")
        t_done = sem("t_done")
        z_done = sem("z_done")
        o_done = sem("o_done")
        oT_done = sem("oT_done")
        xhi_done = sem("xhi_done")
        gelu_done = sem("gelu_done")
        exp_done = sem("exp_done")
        pt_hi_done = sem("pt_hi_done")
        q_hi_done = sem("q_hi_done")
        lat_hi_done = sem("lat_hi_done")
        zhi_done = sem("zhi_done")
        wsplit_hi = sem("wsplit_hi")
        dve_chain = sem("dve_chain")
        ln_in = sem("ln_in")
        norm_in = sem("norm_in")
        arg_in = sem("arg_in")
        norm_done = sem("norm_done")
        xlo_done = sem("xlo_done")
        w_done = sem("w_done")
        rw_done = sem("rw_done")
        r_done = sem("r_done")
        lat_done = sem("lat_done")
        comb_ready = sem("comb_ready")
        combT_done = sem("combT_done")
        lo_done = sem("lo_done")
        one_done = sem("one_done")
        xup_done = sem("xup_done")
        qev_done = sem("qev_done")
        pt_done = sem("pt_done")
        lat_cur_hi = sem("lat_cur_hi")
        max_done = sem("max_done")
        rec_done = sem("rec_done")
        zlo_done = sem("zlo_done")
        latcur_done = sem("latcur_done")
        oev_done = sem("oev_done")
        xres_done = sem("xres_done")

        def did(n):
            return n + CREDIT

        block = ctx.enter_context(nc.Block())

        SMALL = 7 * 16
        CONSTS = 9
        W_CHUNKS = 8
        HH = HEADS // 2
        PARTS = WT // QT
        LN_SEQ, LN_PART = PASSES, PASSES + BATCH
        LN_PASS = (0, LN_PART + PARTS - 1)
        AHEAD = 2 * FC
        STEP_STATS, STEP_NORM, STEP_T, STEP_XLO, STEP_R = 9, 11, 14, 15, (18, 22)
        STEP_SQ, STEP_ARGS, STEP_NEAR, STEP_SECOND, STEP_WEIGHTS, STEP_COMB = 23, 25, 26, 27, 29, 31
        AB_STEP = (10, 14, 18, 22)
        SEQ_STATS, SEQ_NORM, SEQ_T, SEQ_XLO = 22, 24, 26, 27
        STEP_SUM, STEP_UPDATE = 2, 3
        PART_STATS, PART_NORM, PART_T, PART_XLO = ([3 * j + k for j in range(PARTS)] for k in (1, 2, 3, 4))
        W_ORDER = [(k % 2, k // 2) for k in range(W_CHUNKS)]
        DVE_CHUNKS, POOL_CHUNKS = (0, 2, 4, 6), (1, 3, 5, 7)

        def last_sequence(b0):
            return isinstance(b0, int) and b0 == BATCH - 1

        def slot_job(stage, b0, i):
            if last_sequence(b0):
                at = (PART_STATS, PART_NORM, PART_T, PART_XLO)[stage]
                return (LN_PART + at.index(i), at.index(i), at.index(i)) if i in at else None
            return (LN_SEQ + b0 + 1, b0 + 1, 0) if i == (3, 5, 6, 7)[stage] else None

        def weight_chunk(k):
            layer, pair_of = W_ORDER[k]
            cols = slice(pair_of * WIDE, (pair_of + 1) * WIDE)
            return [w[:].rearrange("p e n -> p (e n)")[:, cols] for w in ((w1_hi, w1_lo), (w2_hi, w2_lo))[layer]]

        def run_slots(eng, slot):
            for i in range(-4, HEADS + 1):
                slot(0, i, lambda u: u >= 0, i > 0)
            with eng.Fori(1, BATCH - 1) as b:
                for i in range(1, HEADS + 1):
                    slot(b, i, lambda u: True, True)
            for i in range(1, HEADS + 4):
                slot(BATCH - 1, i, lambda u: u < HEADS, True)

        def run_passes(eng, rest_of_pass, f):
            with eng.Fori(0, PASSES - 1) as t:
                rest_of_pass(f, t, True)
            rest_of_pass(f, PASSES - 1, False)

        @block.sync
        def _(sp):
            x_t, out_t = (a.rearrange("b (q p) d -> p (b q) d", p=P) for a in (x, out))
            sp.dma_start(x_tok[:, 0:WT, :], x_t[:, 0:WT, :]).then_inc(x_loaded0, 16)
            for k, (layer, pair_of) in enumerate(W_ORDER):
                if k == 6:
                    sp.wait_ge(w_done, did(1))
                if k == 7:
                    sp.wait_ge(wp_done, did(1))
                src = (w1, w2)[layer].rearrange("p e n -> p (e n)")[:, pair_of * WIDE:(pair_of + 1) * WIDE]
                sp.dma_start(stage[k], src).then_inc(staged[k], 16)
            sp.dma_start(x_tok[:, WT:TILES, :], x_t[:, WT:TILES, :]).then_inc(x_loaded, 16)

            def spread_comb(p):
                ready, in_dram = sp.snap(did(p + 1)), sp.snap(16 * (p + 1))
                read = sp.snap(16 * (E // 2) * p + CREDIT)
                free = [sp.snap(did(p * E + e)) for e in range(E)]
                sp.wait_ge(combT_done, ready)
                for k in range(2):
                    sp.wait_ge(comb_loaded[k], read)
                sp.dma_start(comb_dram, comb_T).then_inc(comb_stored, 16)
                sp.wait_ge(comb_stored, in_dram)
                rows = comb_dram.rearrange("(e t) p -> e (t p)", e=E)
                for e in range(E):
                    sp.wait_ge(one_done, free[e])
                    sp.dma_start(comb_b[:, e % 2, :], rows[e:e + 1, :].broadcast_to([P, WIDE])) \
                        .then_inc(comb_loaded[e % 2], 16)

            for k in range(2):
                sp.sem_inc(comb_loaded[k], CREDIT)
            sp.wait_ge(w_done, did(len(DVE_CHUNKS) - 1))
            sp.wait_ge(wp_done, did(len(POOL_CHUNKS) - 1))
            with sp.Fori(0, 2 * PASSES) as p:
                spread_comb(p)

            def store(t):
                sp.wait_ge(xup_done, did(PASSES + t + 1))
                sp.dma_start(out_t[:, t * WT:(t + 1) * WT, :], x_tok[:, t * WT:(t + 1) * WT, :]).then_inc(stored, 16)

            for t in range(PASSES):
                store(t)
            sp.wait_ge(stored, 16 * PASSES)

        @block.gpsimd
        def _(pool):
            nc.gpsimd.memset(ident[:], 0.0).then_inc(consts_ready, 1)
            nc.gpsimd.memset(causal_bf[:], 0.0).then_inc(consts_ready, 1)
            nc.gpsimd.memset(ones[:], 1.0).then_inc(consts_ready, 1)
            nc.gpsimd.memset(powers[:, 0:1], -0.5).then_inc(consts_ready, 1)
            nc.gpsimd.memset(powers[:, 1:2], 0.5).then_inc(consts_ready, 1)
            nc.gpsimd.iota(rank[:], pattern=[[-1, E]], base=E, channel_multiplier=0,
                           allow_small_or_imprecise_dtypes=True).then_inc(consts_ready, 1)
            pool.wait_ge(consts_ready, 2)
            nc.gpsimd.affine_select(out=ident[:], in_=ident[:], compare_op=ALU.not_equal, fill=1.0, base=0,
                                    pattern=[[-1, P]], channel_multiplier=1).then_inc(consts_ready, 1)
            nc.gpsimd.affine_select(out=causal_bf[:], in_=causal_bf[:], compare_op=ALU.is_ge, fill=-1e30, base=0,
                                    pattern=[[-1, P]], channel_multiplier=1).then_inc(consts_ready, 1)
            pool.wait_ge(consts_ready, 8)
            nc.gpsimd.tensor_copy(ident_bf[:], ident[:]).then_inc(consts_ready, 1)

            def power(dst, src, which):
                n = src.shape[-1]
                return nc.gpsimd.tensor_tensor(dst, src, powers[0:src.shape[0], which:which + 1].broadcast_to([src.shape[0], n]),
                                               ALU.pow)

            def ln_power(n, tiles):
                pool.wait_ge(ln_in, did(n + 1))
                power(rstd[:, 0:tiles], var_eps[:, 0:tiles], 0).then_inc(ln_root, 1)

            def norm_power(p):
                pool.wait_ge(norm_in, did(1 + p + 1))
                power(tok_s[:, 1, :], tok_s[:, 7, :], 0).then_inc(norm_root, 1)

            def arg_power(p):
                pool.wait_ge(arg_in, did(p + 1))
                power(tok_2[:, 2, :, :].rearrange("p a b -> p (a b)"), tok_2[:, 1, :, :].rearrange("p a b -> p (a b)"), 1) \
                    .then_inc(arg_root, 1)

            def split_weights(k):
                pool.wait_ge(wsplit_hi, did(k + 1))
                hi, lo = weight_chunk(k)
                nc.gpsimd.tensor_tensor(lo, stage[k], hi.bitcast(F32), ALU.subtract).then_inc(wp_done, 1)

            def load_ab(weights):
                for j, w in enumerate(weights):
                    for hh in range(2):
                        pool.dma_start(work[hh * HD:(hh + 1) * HD, j * WIDE:(j + 1) * WIDE].rearrange("p (h d) -> p h d", d=D),
                                       w[:, hh * HH:(hh + 1) * HH, :]).then_inc(ab_staged, 16)

            def add(p, e):
                pool.wait_ge(one_done, did(p * E + e + 1))
                nc.gpsimd.tensor_tensor(y_acc, y_acc, y_one, ALU.add).then_inc(acc_done, 1)
                pool.wait_ge(acc_done, did(p * (E - 1) + e))

            def rest_of_pass(f, t, prepare):
                p = f * PASSES + t
                for e in range(1, E):
                    add(p, e)
                    if prepare and e == 1:
                        ln_power(LN_PASS[f] + t + 1, WT)
                    if prepare and e == 4:
                        norm_power(p + 1)
                    if prepare and e == 5:
                        arg_power(p + 1)
                    if f == 0 and not prepare and e == 2:
                        pool.wait_ge(prep_mm, did(2 + 2))
                        load_ab((wuv_t, w_out))
                    if f == 0 and not prepare and e == 4:
                        ln_power(LN_SEQ, QT)

            def attention_slot(b0, i, live, prepare):
                if live(i + 2):
                    n, k = b0 * HEADS + i + 2, (i + 2) % 2
                    pool.wait_ge(rec_done, did(n + 1))
                    for j, cols in ((0, slice(0, P)), (1, slice(P, PC))):
                        rec = row_rec[:, k, j:j + 1].broadcast_to([P, cols.stop - cols.start])
                        last = nc.gpsimd.tensor_tensor(p_ring[k][:, cols], p_ring[k][:, cols], rec, ALU.mult)
                    last.then_inc(pn_done, 1)
                job = slot_job(0, b0, i) if prepare else None
                if job:
                    ln_power(job[0], QT)

            for own in (ln_root, norm_root, arg_root, wp_done, acc_done, pn_done):
                pool.sem_inc(own, CREDIT)
            ln_power(0, WT)
            pool.wait_ge(norm_in, did(1))
            power(cent_s[:, 1:2], cent_s[:, 0:1], 0).then_inc(norm_root, 1)
            for k in POOL_CHUNKS[:-1]:
                split_weights(k)
            norm_power(0)
            arg_power(0)
            split_weights(POOL_CHUNKS[-1])
            pool.wait_ge(wp_done, did(len(POOL_CHUNKS)))
            pool.wait_ge(w_done, did(len(DVE_CHUNKS)))
            load_ab((wq_t, wuk_t))
            run_passes(pool, rest_of_pass, 0)
            run_slots(pool, attention_slot)
            norm_power(PASSES)
            arg_power(PASSES)
            run_passes(pool, rest_of_pass, 1)

        @block.tensor
        def _(pe):
            for own in (xt_ready, prep_mm, route_mm, lat_mm, l1_done, hi_used, l2_done, combT_mm, accT_done, q_done,
                        s_done, t_done, z_done, o_done, oT_done):
                pe.sem_inc(own, CREDIT)
            pe.wait_ge(consts_ready, CONSTS)

            def transpose_x(n, dst, tiles, at=0):
                pe.wait_ge(norm_done, did(n + 1))
                for i in range(tiles):
                    last = nc.tensor.transpose(dst[:, i * P:(i + 1) * P], xn[:, at + i, :], ident[:])
                last.then_inc(xt_ready, 1)

            def prepare_router():
                pe.wait_ge(small_loaded, SMALL)
                pe.wait_ge(rw_done, did(1))
                nc.tensor.transpose(bank[5][:, 0:E], cent, ident[0:E, 0:E]).then_inc(prep_mm, 1)
                pe.wait_ge(rw_done, did(2))
                nc.tensor.matmul(bank[4][:, 0:E], ones[:].broadcast_to([P, P]), cent_sq[:], start=True, stop=True)
                nc.tensor.matmul(bank[4][:, P:P + E], wp_t_sb, cent_t[:], start=True, stop=True)
                bp_wide = bp_col[:].broadcast_to([P, P])
                nc.tensor.matmul(bank[4][:, 2 * P:3 * P], bp_wide, ident[:], start=True, stop=True)
                nc.tensor.matmul(bank[4][:, 3 * P:3 * P + E], bp_wide, cent_t[:], start=True, stop=True) \
                    .then_inc(prep_mm, 1)

            def route(half, at):
                for i in range(WT // 2):
                    dst = at[:, (i // 2) * HALF + (i % 2) * R_COLS:(i // 2) * HALF + (i % 2 + 1) * R_COLS]
                    n = half * (WT // 2) + i
                    last = nc.tensor.matmul(dst, xT[:, n * P:(n + 1) * P], router_w[:], start=True, stop=True)
                last.then_inc(route_mm, 1)

            def prepare_ab(k, dst):
                pe.wait_ge(ab_staged, 16 * 4 * (k // 2 + 1))
                at = k % 2 * HD
                for h in range(HH):
                    last = nc.tensor.matmul(dst[:, h * D:(h + 1) * D], work[at:at + HD, h * D:(h + 1) * D],
                                            work[at:at + HD, WIDE + h * D:WIDE + (h + 1) * D], start=True, stop=True)
                last.then_inc(prep_mm, 1)

            def layer1(f, t, s):
                e, c = s // FC, s % FC
                pe.wait_ge(gelu_done, did((f * PASSES + t) * STEPS + s - 1))
                w_hi, w_lo = (w[:, e, c * P:(c + 1) * P] for w in (w1_hi, w1_lo))
                dst = h_ps[s % 2]
                for w, m, first, end in ((w_hi, xhi, True, False), (w_hi, xlo, False, False), (w_lo, xhi, False, True)):
                    for j in range(2):
                        last = nc.tensor.matmul(dst[:, j * HALF:(j + 1) * HALF], w,
                                                m[:, bass.ds(t * WIDE + j * HALF, HALF)], start=first, stop=end)
                last.then_inc(l1_done, 1)

            def layer2_hi(p, s):
                e, c = s // FC, s % FC
                pe.wait_ge(gelu_done, did(p * STEPS + s + 1))
                if c == 0:
                    pe.wait_ge(one_done, did(p * E + e - 1))
                for n, w in enumerate((w2_hi, w2_lo)):
                    for j in range(2):
                        last = nc.tensor.matmul(y_ps[e % 2][:, j * HALF:(j + 1) * HALF], w[:, e, c * D:(c + 1) * D],
                                                ring_hi[:, s % 2, j * HALF:(j + 1) * HALF],
                                                start=c == 0 and n == 0, stop=False)
                last.then_inc(hi_used, 1)

            def layer2_lo(p, s):
                e, c = s // FC, s % FC
                pe.wait_ge(lo_done, did(p * STEPS + s + 1))
                for j in range(2):
                    last = nc.tensor.matmul(y_ps[e % 2][:, j * HALF:(j + 1) * HALF], w2_hi[:, e, c * D:(c + 1) * D],
                                            ring_lo[:, s % 2, j * HALF:(j + 1) * HALF], start=False, stop=c == FC - 1)
                last.then_inc(l2_done, 1)

            def transpose_comb(dst):
                nc.tensor.transpose(dst[0:E * WT, 0:P], comb_next[:].rearrange("p e t -> p (e t)"), ident[:]) \
                    .then_inc(combT_mm, 1)

            def transpose_sum(p, dst):
                pe.wait_ge(acc_done, did((p + 1) * (E - 1)))
                for i in range(WT):
                    last = nc.tensor.transpose(dst[:, i * P:(i + 1) * P], y_acc[:, i * P:(i + 1) * P], ident[:])
                last.then_inc(accT_done, 1)

            def rest_of_pass(f, t, prepare):
                p = f * PASSES + t
                ab = f == 0 and not prepare
                n_ln = LN_PASS[f] + t + 1
                for s in range(AHEAD, STEPS):
                    e, spare = s // FC, y_ps[(s // FC + 1) % 2]
                    busy = (STEP_T,) + STEP_R + (STEP_COMB,) if prepare else AB_STEP + (SEQ_T,) if ab else ()
                    if s in busy:
                        pe.wait_ge(one_done, did(p * E + e))
                    if prepare and s == STEP_COMB:
                        pe.wait_ge(comb_ready, did(p + 2))
                    if s < STEPS - 1:
                        layer1(f, t, s + 1)
                    elif prepare:
                        layer1(f, t + 1, 0)
                    if s in busy:
                        if ab and s == SEQ_T:
                            transpose_x(LN_SEQ, spare, QT)
                        elif ab:
                            prepare_ab(AB_STEP.index(s), spare)
                        elif s == STEP_T:
                            transpose_x(n_ln, spare, WT)
                        elif s in STEP_R:
                            half = STEP_R.index(s)
                            pe.wait_ge(xlo_done, did(n_ln + 1))
                            route(half, spare)
                        else:
                            transpose_comb(spare)
                    if prepare and s == (STEP_T // FC + 1) * FC:
                        pe.wait_ge(xlo_done, did(n_ln + 1))
                    for half in range(2):
                        if prepare and s == (STEP_R[half] // FC + 1) * FC:
                            pe.wait_ge(r_done, did(2 * (p + 1) + half + 1))
                    if ab and s - 2 in AB_STEP:
                        pe.wait_ge(w_done, did(len(DVE_CHUNKS) + AB_STEP.index(s - 2) + 1))
                    if ab and s - 2 == SEQ_T:
                        pe.wait_ge(xlo_done, did(LN_SEQ + 1))
                    layer2_hi(p, s)
                    layer2_lo(p, s - 1)
                if not prepare:
                    layer2_lo(p, STEPS - 1)
                    return
                for s in range(AHEAD):
                    layer1(f, t + 1, s + 1)
                    if s == 0:
                        pe.wait_ge(combT_done, did(p + 2))
                    if s == STEP_SUM:
                        transpose_sum(p, y_ps[1])
                    if s == FC:
                        pe.wait_ge(xup_done, did(p + 1))
                    layer2_hi(p + 1, s)
                    if s > 0:
                        layer2_lo(p + 1, s - 1)
                    else:
                        layer2_lo(p, STEPS - 1)

            def latent(dst, b, token_major):
                if not token_major:
                    nc.tensor.matmul(dst, w_down_sb[:], xT[:, 0:SEQ], start=True, stop=True).then_inc(lat_mm, 1)
                else:
                    for i in range(QT):
                        last = nc.tensor.matmul(dst[:, i * P:(i + 1) * P], xT[:, i * P:(i + 1) * P], w_down_sb[:],
                                                start=True, stop=True)
                    last.then_inc(lat_mm, 1)

            def attention_slot(b0, i, live, prepare):
                def unit(u):
                    return b0 * HEADS + u, u % HEADS, b0 + u // HEADS
                if live(i + 3):
                    n, h, b = unit(i + 3)
                    pe.wait_ge(qev_done, did(n + 1))
                    pe.wait_ge(exp_done, did(n - 1))
                    if h == 0:
                        pe.wait_ge(lat_done, did(2 * b + 1))
                    dst, q, (q_hi, q_lo) = s_bank[(i + 3) % 2], q_ring[(i + 3) % 2], q_split[(i + 3) % 2]
                    lat_hi, lat_lo = lat_T_split(b)
                    nc.tensor.matmul(dst[:, P:PC], q_hi, lat_lo, start=True, stop=False, skip_group_check=True)
                    nc.tensor.matmul(dst[:, P:PC], q_lo, lat_hi, start=False, stop=False, skip_group_check=True)
                    nc.tensor.matmul(dst[:, P:PC], q_hi, lat_hi, start=False, stop=False, skip_group_check=True)
                    nc.tensor.matmul(dst[:, 0:P], q, lat_T[:, bass.ds(b * P, P)], start=False, stop=False,
                                     skip_group_check=True)
                    nc.tensor.matmul(dst.rearrange("p (t k) -> p t k", t=QT)[:, :, 0:P], ident_bf[:],
                                     causal_bf[:].unsqueeze(1).broadcast_to([P, QT, P]), start=False, stop=True,
                                     skip_group_check=True).then_inc(s_done, 1)
                if live(i + 4):
                    n, h, b = unit(i + 4)
                    pe.wait_ge(qev_done, did(n))
                    if h == 0:
                        pe.wait_ge(xlo_done, did(LN_SEQ + b + 1))
                    m_hi, m_lo = (m[:, bass.ds(b * SEQ, SEQ)] for m in (xhi, xlo))
                    nc.tensor.matmul(q_bank[:, 0:SEQ], a_hi[:, h, :], m_lo, start=True, stop=False)
                    nc.tensor.matmul(q_bank[:, 0:SEQ], a_lo[:, h, :], m_hi, start=False, stop=False)
                    nc.tensor.matmul(q_bank[:, 0:SEQ], a_hi[:, h, :], m_hi, start=False, stop=True).then_inc(q_done, 1)
                if i == -1:
                    transpose_sum(PASSES - 1, y_ps[0])
                    pe.wait_ge(xup_done, did(PASSES))
                if live(i - 2):
                    n, h, b = unit(i - 2)
                    pe.wait_ge(zlo_done, did(n + 1))
                    if h == 0:
                        pe.wait_ge(oev_done, did(b))
                    z_hi, z_lo = z_split[i % 2]
                    first, last = h == 0, h == HEADS - 1
                    nc.tensor.matmul(o_bank[:, 0:SEQ], b_lo[:, h, :], z_hi, start=first, stop=False)
                    nc.tensor.matmul(o_bank[:, 0:SEQ], b_hi[:, h, :], z_lo, start=False, stop=False)
                    nc.tensor.matmul(o_bank[:, 0:SEQ], b_hi[:, h, :], z_hi, start=False, stop=last).then_inc(o_done, 1)
                if live(i + 1):
                    n, h, b = unit(i + 1)
                    pe.wait_ge(pn_done, did(n + 1))
                    pe.wait_ge(pt_done, did(n - 1))
                    for k in range(3):
                        last = nc.tensor.transpose(t_bank[(i + 1) % 2][:, k * P:(k + 1) * P],
                                                   p_ring[(i + 1) % 2][:, k * P:(k + 1) * P], ident[:])
                    last.then_inc(t_done, 1)
                z, beside = z_bank[i % 2][:, 0:SEQ], z_bank[i % 2][:, SEQ:2 * SEQ]
                if live(i):
                    n, h, b = unit(i)
                    pe.wait_ge(pt_hi_done, did(n + 1))
                    pe.wait_ge(zlo_done, did(n - 1))
                if i % HEADS == 2 and live(i - 3):
                    b = unit(i - 3)[2]
                    pe.wait_ge(oev_done, did(b + 1))
                    if not live(i):
                        pe.wait_ge(zlo_done, did(UNITS))
                    for j in range(QT):
                        last = nc.tensor.transpose(beside[:, j * P:(j + 1) * P], o_sb[:, j * P:(j + 1) * P], ident[:])
                    last.then_inc(oT_done, 1)
                job = slot_job(2, b0, i) if prepare else None
                if job:
                    transpose_x(job[0], beside, QT, job[2] * QT)
                if prepare and not last_sequence(b0) and i == 8:
                    pe.wait_ge(xlo_done, did(LN_SEQ + b0 + 2))
                    latent(beside, b0 + 1, False)
                if prepare and not last_sequence(b0) and i == 9:
                    latent(beside, b0 + 1, True)
                if live(i):
                    n, h, b = unit(i)
                    if h == 0:
                        pe.wait_ge(latcur_done, did(b + 1))
                    pt, (pt_hi, pt_lo), (c_hi, c_lo) = pt_ring[i % 2], pt_split[i % 2], lat_cur_split
                    nc.tensor.matmul(z, c_lo, pt_hi, start=True, stop=False)
                    nc.tensor.matmul(z, c_hi, pt_hi, start=False, stop=False)
                    nc.tensor.matmul(z[:, P:SEQ], lat_cur, pt, start=False, stop=False)
                    pe.wait_ge(pt_done, did(n + 1))
                    nc.tensor.matmul(z, c_hi, pt_lo, start=False, stop=True).then_inc(z_done, 1)

            def begin(f):
                if f == 0:
                    transpose_x(0, y_ps[1], WT)
                    prepare_router()
                    pe.wait_ge(xlo_done, did(1))
                    pe.wait_ge(w_done, did(1))
                else:
                    pe.wait_ge(oev_done, did(BATCH))
                layer1(f, 0, 0)
                if f == 0:
                    pe.wait_ge(rw_done, did(3))
                else:
                    pe.wait_ge(xres_done, did(BATCH))
                route(0, y_ps[1])
                if f == 1:
                    pe.wait_ge(exp_done, did(UNITS))
                layer1(f, 0, 1)
                pe.wait_ge(r_done, did(2 * f * PASSES + 1))
                route(1, y_ps[1])
                for s in range(AHEAD):
                    if 0 < s < AHEAD - 1:
                        layer1(f, 0, s + 1)
                    if s == 0 and f == 0:
                        pe.wait_ge(wp_done, did(1))
                    if s == 0 and f == 1:
                        pe.wait_ge(pt_done, did(UNITS))
                    if s == FC:
                        pe.wait_ge(r_done, did(2 * (f * PASSES + 1)))
                    if s == AHEAD - 1:
                        pe.wait_ge(comb_ready, did(f * PASSES + 1))
                        transpose_comb(h_ps[AHEAD % 2])
                        if f == 0:
                            pe.wait_ge(w_done, did(2))
                        pe.wait_ge(combT_done, did(f * PASSES + 1))
                        layer1(f, 0, AHEAD)
                    layer2_hi(f * PASSES, s)
                    if s > 0:
                        layer2_lo(f * PASSES, s - 1)

            begin(0)
            pe.wait_ge(w_done, did(len(DVE_CHUNKS)))
            pe.wait_ge(wp_done, did(len(POOL_CHUNKS)))
            run_passes(pe, rest_of_pass, 0)
            latent(s_bank[0][:, 0:SEQ], 0, False)
            latent(s_bank[1][:, 0:SEQ], 0, True)
            run_slots(pe, attention_slot)
            begin(1)
            run_passes(pe, rest_of_pass, 1)
            transpose_sum(2 * PASSES - 1, y_ps[0])

        @block.scalar
        def _(act):
            for own in (xhi_done, gelu_done, exp_done, pt_hi_done, q_hi_done, lat_hi_done, zhi_done, wsplit_hi):
                act.sem_inc(own, CREDIT)
            A = nc.scalar.activation

            def x_hi(n, src, col, cols):
                act.wait_ge(xt_ready, did(n + 1))
                A(xhi[:, bass.ds(col, cols)], src, ACT.Copy).then_inc(xhi_done, 1)

            def split_weights(k):
                act.wait_ge(staged[k], 16)
                A(weight_chunk(k)[0], stage[k], ACT.Copy).then_inc(wsplit_hi, 1)

            def split_ab(k, src):
                act.wait_ge(prep_mm, did(2 + k + 1))
                dst = (a_hi, b_hi)[k // 2][:, (k % 2) * HH:(k % 2 + 1) * HH, :].rearrange("p h d -> p (h d)")
                A(dst, src, ACT.Copy, scale=(HD ** -0.5, 1.0)[k // 2]).then_inc(wsplit_hi, 1)

            def step(p, s):
                e, c = s // FC, s % FC
                n = p * STEPS + s
                act.wait_ge(l1_done, did(n + 1))
                act.wait_ge(lo_done, did(n - 1))
                A(h_ring[:, s % 2, :], h_ps[s % 2][:], ACT.Gelu, bias=b1_sb[:, e, c:c + 1])
                act.wait_ge(hi_used, did(n - 1))
                A(ring_hi[:, s % 2, :], h_ps[s % 2][:], ACT.Gelu, bias=b1_sb[:, e, c:c + 1]).then_inc(gelu_done, 1)

            def rest_of_pass(f, t, prepare):
                p = f * PASSES + t
                ab = f == 0 and not prepare
                for s in range(AHEAD, STEPS):
                    step(p, s)
                    spare = y_ps[(s // FC + 1) % 2]
                    if prepare and s == STEP_T:
                        x_hi(LN_PASS[f] + t + 1, spare[:], (t + 1) * WIDE, WIDE)
                    if ab and s in AB_STEP:
                        split_ab(AB_STEP.index(s), spare[:])
                    if ab and s == SEQ_T:
                        x_hi(LN_SEQ, spare[:, 0:SEQ], 0, SEQ)
                if prepare:
                    for s in range(AHEAD):
                        step(p + 1, s)

            def latent_hi(b, src):
                act.wait_ge(lat_mm, did(2 * b + 1))
                A(lat_T_split(b)[0], src, ACT.Copy).then_inc(lat_hi_done, 1)

            def attention_slot(b0, i, live, prepare):
                def unit(u):
                    return b0 * HEADS + u
                if live(i - 1):
                    n, k = unit(i - 1), (i - 1) % 2
                    act.wait_ge(z_done, did(n + 1))
                    act.wait_ge(o_done, did(n - 1))
                    A(ring_hi[:, k, 0:SEQ], z_bank[k][:, 0:SEQ], ACT.Copy).then_inc(zhi_done, 1)
                job = slot_job(3, b0, i) if prepare else None
                if job:
                    x_hi(job[0], z_bank[(i - 1) % 2][:, SEQ:2 * SEQ], job[1] * SEQ, SEQ)
                if prepare and not last_sequence(b0) and i == 9:
                    latent_hi(b0 + 1, z_bank[(i - 1) % 2][:, SEQ:2 * SEQ])
                if live(i + 4):
                    n, k = unit(i + 4), i % 2
                    act.wait_ge(q_done, did(n + 1))
                    act.wait_ge(s_done, did(n - 1))
                    A(q_split[k][0], q_bank[:, P:SEQ], ACT.Copy).then_inc(q_hi_done, 1)
                if live(i + 1):
                    n, k = unit(i + 1), (i + 1) % 2
                    act.wait_ge(t_done, did(n + 1))
                    act.wait_ge(z_done, did(n - 1))
                    A(pt_split[k][0], t_bank[k][:, 0:SEQ], ACT.Copy)
                    A(pt_ring[k], t_bank[k][:, SEQ:PC], ACT.Copy).then_inc(pt_hi_done, 1)
                if live(i + 3):
                    n, k = unit(i + 3), (i + 3) % 2
                    act.wait_ge(max_done, did(n + 1))
                    act.wait_ge(t_done, did(n - 1))
                    A(p_ring[k][:, 0:P], s_bank[k][:, 0:P], ACT.Exp, bias=neg_max[:, k, 0:1], accum_out=row_sum[:, k, 0:1])
                    A(p_ring[k][:, P:PC], s_bank[k][:, P:PC], ACT.Exp, bias=neg_max[:, k, 1:2],
                      accum_out=row_sum[:, k, 1:2]).then_inc(exp_done, 1)

            for dst, src in ((cent, centroids), (bp_col[:], bp), (b1_sb[:], b1), (b2_sb[:], b2),
                             (router_w[:, 0:D], wp), (wp_t_sb, wp_t), (w_down_sb[:], w_down)):
                act.dma_start(dst, src).then_inc(small_loaded, 16)
            x_hi(0, y_ps[1][:], 0, WIDE)
            act.wait_ge(small_loaded, SMALL)
            for k in range(W_CHUNKS - 2):
                split_weights(k)
            for s in range(AHEAD):
                step(0, s)
                if s < 2:
                    split_weights(W_CHUNKS - 2 + s)
            act.wait_ge(w_done, did(len(DVE_CHUNKS)))
            act.wait_ge(wp_done, did(len(POOL_CHUNKS)))
            run_passes(act, rest_of_pass, 0)
            latent_hi(0, s_bank[0][:, 0:SEQ])
            run_slots(act, attention_slot)
            for s in range(AHEAD):
                step(PASSES, s)
            run_passes(act, rest_of_pass, 1)

        @block.vector
        def _(dve):
            for own in (dve_chain, ln_in, norm_in, arg_in, norm_done, xlo_done, w_done, rw_done, r_done, lat_done,
                        comb_ready, combT_done, lo_done, one_done, xup_done, qev_done,
                        pt_done, lat_cur_hi, max_done, rec_done, zlo_done, latcur_done, oev_done, xres_done):
                dve.sem_inc(own, CREDIT)
            V = nc.vector
            PASS_LINKS, SEQ_LINKS = 34, 2
            links = [0, 0]
            before_moe, before_attention = [0, 0], [0]

            def link(instruction):
                links[1] = links[1] + 1
                instruction.then_inc(dve_chain, 1)
                dve.wait_ge(dve_chain, did(links[0] + links[1]))

            def ln_stats(tile, tiles):
                for i in range(tiles):
                    last = V.bn_stats(stats[:, i, :], x_flat[:, bass.ds((tile + i) * D, D)])
                link(last)
                V.tensor_copy(after_wait[:], stats[:, 0, 0:1])
                for i in range(tiles):
                    last = V.bn_aggr(mean_var[:, i, :], stats[:, i, :])
                link(last)
                V.tensor_scalar(var_eps[:, 0:tiles], mean_var[:, 0:tiles, 1], LN_EPS, None, ALU.add).then_inc(ln_in, 1)

            def ln_apply(n, tile, tiles, at=0):
                dve.wait_ge(ln_root, did(n + 1))
                for i in range(tiles):
                    last = V.tensor_scalar(xn[:, at + i, :], x_flat[:, bass.ds((tile + i) * D, D)], mean_var[:, i, 0:1],
                                           rstd[:, i:i + 1], ALU.subtract, ALU.mult)
                last.then_inc(norm_done, 1)

            def x_lo(n, src, col, cols, at=0):
                dve.wait_ge(xhi_done, did(n + 1))
                V.tensor_copy(xT[:, at:at + cols], src)
                V.tensor_tensor(xlo[:, bass.ds(col, cols)], src, xhi[:, bass.ds(col, cols)].bitcast(F32), ALU.subtract) \
                    .then_inc(xlo_done, 1)

            def per_token(v):
                return v.unsqueeze(2).broadcast_to([P, WT, E])

            def per_expert(v):
                return v.unsqueeze(1).broadcast_to([P, WT, E])

            def route_evacuate(p, half, src):
                dve.wait_ge(route_mm, did(2 * p + half + 1))
                got = src[:].rearrange("p (b c) -> p b c", b=2)[:, :, 0:2 * R_COLS] \
                    .rearrange("p b (t c) -> p b t c", t=2)
                n = WT // 2
                r = xn[:, half * n:(half + 1) * n, :].rearrange("p (b t) d -> p b t d", b=2)
                d = r_dot[:, half * n:(half + 1) * n, :].rearrange("p (b t) e -> p b t e", b=2)
                for b in range(2):
                    V.tensor_tensor(r[:, b, :, :], got[:, b, :, 0:D], router_b[:, 0:D].unsqueeze(1).broadcast_to([P, 2, D]), ALU.add)
                    last = V.tensor_tensor(d[:, b, :, :], got[:, b, :, D:R_COLS],
                                           router_b[:, D:R_COLS].unsqueeze(1).broadcast_to([P, 2, E]), ALU.add)
                last.then_inc(r_done, 1)

            n2, root, scale, xn2, one_m, m_1, k_1, n2_clip = (tok_s[:, k, :] for k in range(8))

            def route_norms(p):
                dve.wait_ge(r_done, did(2 * (p + 1)))
                link(V.tensor_tensor(xn, xn, xn, ALU.mult))
                link(V.tensor_reduce(n2, xn, AX.X, ALU.add))
                V.tensor_scalar(n2_clip, n2, BALL_EPS * BALL_EPS, None, ALU.max).then_inc(norm_in, 1)

            def route_args(p):
                dve.wait_ge(norm_root, did(1 + p + 1))
                link(V.tensor_scalar(scale, root, MAX_NORM, 1.0, ALU.mult, ALU.min))
                V.tensor_tensor(dot, r_dot, per_token(scale), ALU.mult)
                link(V.tensor_tensor(xn2, scale, scale, ALU.mult))
                link(V.tensor_tensor(xn2, xn2, n2, ALU.mult))
                link(V.tensor_scalar(xn2, xn2, MAX_SQ, None, ALU.min))
                V.scalar_tensor_tensor(arg, dot, -2.0, per_expert(cn2[:, 0, :]), ALU.mult, ALU.add)
                link(V.tensor_scalar(one_m, xn2, -1.0, 1.0, ALU.mult, ALU.add))
                V.tensor_tensor(arg, arg, per_token(xn2), ALU.add)
                link(V.tensor_tensor(den, per_expert(cn2[:, 1, :]), per_token(one_m), ALU.mult))
                link(V.tensor_scalar(den, den, BALL_EPS, None, ALU.add))
                link(V.reciprocal(den, den))
                link(V.scalar_tensor_tensor(arg, arg, 0.0, den, ALU.max, ALU.mult))
                link(V.tensor_scalar(arg, arg, 2.0, 1.0, ALU.mult, ALU.add))
                link(V.tensor_scalar(arg, arg, 1.0 + BALL_EPS, None, ALU.max))

            def nearest(sel, values, least):
                link(V.tensor_reduce(least, values, AX.X, ALU.min))
                link(V.tensor_tensor(tmp, values, per_token(least), ALU.is_equal))
                link(V.tensor_tensor(tmp, tmp, per_expert(rank[:]), ALU.mult))
                link(V.tensor_reduce(k_1, tmp, AX.X, ALU.max))
                link(V.tensor_tensor(sel, tmp, per_token(k_1), ALU.is_equal))

            def route_second():
                link(V.scalar_tensor_tensor(den, sel1, 1e30, arg, ALU.mult, ALU.add))
                nearest(sel2, den, tok_2[:, 0, 1, :])
                link(V.tensor_scalar(tok_2[:, 1, :, :], tok_2[:, 0, :, :], 1.0, None, ALU.add))
                V.scalar_tensor_tensor(tok_2[:, 1, :, :], tok_2[:, 0, :, :], -1.0, tok_2[:, 1, :, :], ALU.add, ALU.mult) \
                    .then_inc(arg_in, 1)

            def route_weights(p):
                dve.wait_ge(arg_root, did(p + 1))
                link(V.tensor_tensor(tok_2[:, 0, :, :], tok_2[:, 0, :, :], tok_2[:, 2, :, :], ALU.add))
                link(V.reciprocal(m_1, tok_2[:, 0, 1, :]))
                link(V.tensor_tensor(m_1, m_1, tok_2[:, 0, 0, :], ALU.mult))
                link(V.tensor_scalar(k_1, m_1, 1.0, None, ALU.add))
                link(V.reciprocal(k_1, k_1))
                link(V.tensor_tensor(m_1, m_1, k_1, ALU.mult))
                V.tensor_tensor(sel1, sel1, per_token(k_1), ALU.mult)
                link(V.tensor_tensor(sel2, sel2, per_token(m_1), ALU.mult))
                V.tensor_tensor(comb_next[:].rearrange("p e t -> p t e"), sel1, sel2, ALU.add).then_inc(comb_ready, 1)

            def prepare_router():
                dve.wait_ge(small_loaded, SMALL)
                sq = lat_next[0:E, 0, :]
                link(V.tensor_tensor(sq, cent, cent, ALU.mult))
                link(V.tensor_reduce(cent_s[:, 2:3], sq, AX.X, ALU.add))
                V.tensor_scalar(cent_s[:, 0:1], cent_s[:, 2:3], BALL_EPS * BALL_EPS, None, ALU.max).then_inc(norm_in, 1)
                dve.wait_ge(norm_root, did(1))
                link(V.tensor_scalar(cent_s[:, 3:4], cent_s[:, 1:2], MAX_NORM, 1.0, ALU.mult, ALU.min))
                V.tensor_scalar(cent, cent, cent_s[:, 3:4], None, ALU.mult).then_inc(rw_done, 1)
                dve.wait_ge(prep_mm, did(1))
                link(V.tensor_copy(cent_t[:], bank[5][:, 0:E]))
                V.tensor_tensor(cent_sq[:], cent_t[:], cent_t[:], ALU.mult).then_inc(rw_done, 1)
                dve.wait_ge(prep_mm, did(2))
                link(V.tensor_scalar(cn2[:, 0, :], bank[4][:, 0:E], MAX_SQ, None, ALU.min))
                V.tensor_scalar(cn2[:, 1, :], cn2[:, 0, :], -1.0, 1.0, ALU.mult, ALU.add)
                V.tensor_copy(router_w[:, D:R_COLS], bank[4][:, P:P + E])
                V.tensor_copy(router_b[:], bank[4][:, 2 * P:2 * P + R_COLS]).then_inc(rw_done, 1)

            def split_weights(k):
                dve.wait_ge(wsplit_hi, did(k + 1))
                hi, lo = weight_chunk(k)
                V.tensor_tensor(lo, stage[k], hi.bitcast(F32), ALU.subtract).then_inc(w_done, 1)

            def split_ab(k, src):
                dve.wait_ge(wsplit_hi, did(W_CHUNKS + k + 1))
                hi, lo = (w[:, (k % 2) * HH:(k % 2 + 1) * HH, :].rearrange("p h d -> p (h d)")
                          for w in ((a_hi, a_lo), (b_hi, b_lo))[k // 2])
                V.scalar_tensor_tensor(lo, src, (HD ** -0.5, 1.0)[k // 2], hi.bitcast(F32),
                                       ALU.mult, ALU.subtract).then_inc(w_done, 1)

            def lo_of_step(p, s):
                n = p * STEPS + s
                dve.wait_ge(gelu_done, did(n + 1))
                dve.wait_ge(l2_done, did(n - 1))
                V.tensor_tensor(ring_lo[:, s % 2, :], h_ring[:, s % 2, :], ring_hi[:, s % 2, :].bitcast(F32),
                                ALU.subtract).then_inc(lo_done, 1)

            def fold(p, e):
                dve.wait_ge(l2_done, did(p * STEPS + (e + 1) * FC))
                dve.wait_ge(comb_loaded[e % 2], 16 * (p * (E // 2) + e // 2 + 1) + CREDIT)
                if e > 1:
                    dve.wait_ge(acc_done, did(p * (E - 1) + e - 1))
                V.scalar_tensor_tensor(y_acc if e == 0 else y_one, y_ps[e % 2][:], b2_sb[:, e:e + 1], comb_b[:, e % 2, :],
                                       ALU.add, ALU.mult).then_inc(one_done, 1)

            def comb_evacuate(p, src):
                dve.wait_ge(combT_mm, did(p + 1))
                V.tensor_copy(comb_T, src[0:E * WT, 0:P]).then_inc(combT_done, 1)

            def update_x(p, t, src):
                dve.wait_ge(accT_done, did(p + 1))
                here = x_flat[:, bass.ds(t * WIDE, WIDE)]
                V.scalar_tensor_tensor(here, src, 0.5, here, ALU.mult, ALU.add).then_inc(xup_done, 1)

            def rest_of_pass(f, t, prepare):
                p = f * PASSES + t
                ab = f == 0 and not prepare
                n_ln = LN_PASS[f] + t + 1
                links[:] = before_moe[f] + t * PASS_LINKS, 0
                for s in range(AHEAD, STEPS):
                    lo_of_step(p, s)
                    spare = y_ps[(s // FC + 1) % 2]
                    if s % FC == 0:
                        fold(p, s // FC - 1)
                    if prepare:
                        if s == STEP_STATS:
                            if f == 0:
                                dve.wait_ge(x_loaded, 16)
                            ln_stats((t + 1) * WT, WT)
                        if s == STEP_NORM:
                            ln_apply(n_ln, (t + 1) * WT, WT)
                        if s == STEP_XLO:
                            x_lo(n_ln, spare[:], (t + 1) * WIDE, WIDE)
                        if s in STEP_R:
                            route_evacuate(p + 1, STEP_R.index(s), spare)
                        if s == STEP_SQ:
                            route_norms(p + 1)
                        if s == STEP_ARGS:
                            route_args(p + 1)
                        if s == STEP_NEAR:
                            nearest(sel1, arg, tok_2[:, 0, 0, :])
                        if s == STEP_SECOND:
                            route_second()
                        if s == STEP_WEIGHTS:
                            route_weights(p + 1)
                        if s == STEP_COMB:
                            dve.wait_ge(comb_stored, 16 * (p + 1))
                            comb_evacuate(p + 1, spare)
                    if ab:
                        if s - 1 in AB_STEP:
                            split_ab(AB_STEP.index(s - 1), spare[:])
                        if s == SEQ_STATS:
                            ln_stats(0, QT)
                        if s == SEQ_NORM:
                            ln_apply(LN_SEQ, 0, QT)
                        if s == SEQ_XLO:
                            x_lo(LN_SEQ, spare[:, 0:SEQ], 0, SEQ)
                assert links[1] == (PASS_LINKS if prepare else SEQ_LINKS if ab else 0), links
                if prepare:
                    for s in range(AHEAD):
                        lo_of_step(p + 1, s)
                        if s == 0:
                            fold(p, E - 1)
                        if s == STEP_UPDATE:
                            update_x(p, t, y_ps[1][:])
                        if s == FC:
                            fold(p + 1, 0)
                else:
                    if ab:
                        latent_evacuate(0, s_bank[0][:, 0:SEQ], 0)
                    fold(p, E - 1)
                    if ab:
                        latent_evacuate(0, s_bank[1][:, 0:SEQ], 1)
                    if f == 1:
                        update_x(p, t, y_ps[0][:])

            def begin(f):
                p = f * PASSES
                if f == 0:
                    dve.wait_ge(x_loaded0, 16)
                    ln_stats(0, WT)
                    ln_apply(0, 0, WT)
                    prepare_router()
                    x_lo(0, y_ps[1][:], 0, WIDE)
                    for k in DVE_CHUNKS[:-1]:
                        split_weights(k)
                for half in range(2):
                    route_evacuate(p, half, y_ps[1])
                lo_of_step(p, 0)
                route_norms(p)
                lo_of_step(p, 1)
                route_args(p)
                lo_of_step(p, 2)
                nearest(sel1, arg, tok_2[:, 0, 0, :])
                route_second()
                lo_of_step(p, 3)
                lo_of_step(p, 4)
                route_weights(p)
                lo_of_step(p, 5)
                lo_of_step(p, 6)
                if f == 1:
                    dve.wait_ge(comb_stored, 16 * p)
                comb_evacuate(p, h_ps[AHEAD % 2])
                lo_of_step(p, 7)
                if f == 0:
                    split_weights(DVE_CHUNKS[-1])
                    dve.wait_ge(wp_done, did(2))
                dve.wait_ge(l2_done, did(p * STEPS + FC))
                V.tensor_scalar(y_acc, y_ps[0][:], b2_sb[:, 0:1], None, ALU.add).then_inc(one_done, 1)
                dve.wait_ge(one_done, did(p * E + 1))
                dve.wait_ge(comb_loaded[0], 16 * (p * (E // 2) + 1) + CREDIT)
                V.tensor_tensor(y_acc, y_acc, comb_b[:, 0, :], ALU.mult)

            def latent_evacuate(b, src, token_major):
                if token_major:
                    dve.wait_ge(lat_mm, did(2 * b + 2))
                    V.tensor_copy(lat_next[:].rearrange("p q d -> p (q d)"), src).then_inc(lat_done, 1)
                else:
                    dve.wait_ge(lat_hi_done, did(b + 1))
                    hi, lo = lat_T_split(b)
                    V.tensor_copy(lat_T[:, bass.ds(b * P, P)], src[:, 0:P])
                    V.tensor_tensor(lo, src, hi.bitcast(F32), ALU.subtract).then_inc(lat_done, 1)

            def attention_slot(b0, i, live, prepare):
                def unit(u):
                    return b0 * HEADS + u, b0 + u // HEADS
                if i % HEADS == 0 and live(i):
                    n, b = unit(i)
                    dve.wait_ge(lat_done, did(2 * b + 2))
                    dve.wait_ge(z_done, did(n))
                    hi, lo = lat_cur_split
                    V.tensor_copy(hi, lat_next[:, 0, :]).then_inc(lat_cur_hi, 1)
                    V.tensor_copy(lat_cur, lat_next[:, 1, :])
                    dve.wait_ge(lat_cur_hi, did(b + 1))
                    V.tensor_tensor(lo, lat_next[:, 0, :], hi.bitcast(F32), ALU.subtract).then_inc(latcur_done, 1)
                if live(i + 2):
                    n, k = unit(i + 2)[0], (i + 2) % 2
                    dve.wait_ge(exp_done, did(n + 1))
                    dve.wait_ge(pn_done, did(n - 1))
                    V.reciprocal(row_rec[:, k, :], row_sum[:, k, :]).then_inc(rec_done, 1)
                if live(i + 3):
                    n, k = unit(i + 3)[0], (i + 3) % 2
                    dve.wait_ge(s_done, did(n + 1))
                    dve.wait_ge(exp_done, did(n - 1))
                    V.tensor_reduce(neg_max[:, k, 0:1], s_bank[k][:, 0:P], AX.X, ALU.max, negate=True)
                    V.tensor_reduce(neg_max[:, k, 1:2], s_bank[k][:, P:PC], AX.X, ALU.max, negate=True) \
                        .then_inc(max_done, 1)
                if live(i + 4):
                    n, k = unit(i + 4)[0], i % 2
                    dve.wait_ge(q_hi_done, did(n + 1))
                    hi, lo = q_split[k]
                    V.tensor_copy(q_ring[k], q_bank[:, 0:P])
                    V.tensor_tensor(lo, q_bank[:, P:SEQ], hi.bitcast(F32), ALU.subtract).then_inc(qev_done, 1)
                if live(i - 1):
                    n, k = unit(i - 1)[0], (i - 1) % 2
                    dve.wait_ge(zhi_done, did(n + 1))
                beside = z_bank[(i - 1) % 2][:, SEQ:2 * SEQ]
                if i % HEADS == 3 and live(i - 4):
                    b = unit(i - 4)[1]
                    dve.wait_ge(oT_done, did(b + 1))
                    here = x_flat[:, bass.ds(b * SEQ, SEQ)]
                    V.tensor_tensor(here, here, beside, ALU.add).then_inc(xres_done, 1)
                job = slot_job(3, b0, i) if prepare else None
                if job:
                    x_lo(job[0], beside, job[1] * SEQ, SEQ, job[2] * SEQ)
                if prepare and not last_sequence(b0) and i in (9, 10):
                    latent_evacuate(b0 + 1, beside, i - 9)
                if live(i - 1):
                    n, k = unit(i - 1)[0], (i - 1) % 2
                    dve.wait_ge(o_done, did(n - 1))
                    V.tensor_tensor(ring_lo[:, k, 0:SEQ], z_bank[k][:, 0:SEQ], ring_hi[:, k, 0:SEQ].bitcast(F32),
                                    ALU.subtract).then_inc(zlo_done, 1)
                if i % HEADS == 1 and live(i - 2):
                    n, b = unit(i - 2)
                    dve.wait_ge(o_done, did(n + 1))
                    dve.wait_ge(oT_done, did(b))
                    V.tensor_copy(o_sb, o_bank[:, 0:SEQ]).then_inc(oev_done, 1)
                if i == -1:
                    update_x(PASSES - 1, PASSES - 1, y_ps[0][:])
                if live(i + 1):
                    n, k = unit(i + 1)[0], (i + 1) % 2
                    dve.wait_ge(pt_hi_done, did(n + 1))
                    hi, lo = pt_split[k]
                    V.tensor_tensor(lo, t_bank[k][:, 0:SEQ], hi.bitcast(F32), ALU.subtract).then_inc(pt_done, 1)
                job = slot_job(0, b0, i) if prepare else None
                if job:
                    links[:] = before_attention[0] + (job[0] - LN_SEQ - 1) * SEQ_LINKS, 0
                    ln_stats(job[1] * QT, QT)
                job = slot_job(1, b0, i) if prepare else None
                if job:
                    ln_apply(job[0], job[1] * QT, QT, job[2] * QT)

            begin(0)
            before_moe[0] = sum(links)
            run_passes(dve, rest_of_pass, 0)
            before_attention[0] = sum(links)
            run_slots(dve, attention_slot)
            begin(1)
            before_moe[1] = sum(links)
            run_passes(dve, rest_of_pass, 1)
    return nc


_OUT = (16, 256, 128)


def kernel(**inputs):
    import numpy as _np
    import concourse.bacc as _bacc
    from concourse import mybir as _mybir
    from concourse.bass_utils import run_bass_kernel_spmd as _run

    a = {k: _np.asarray(v) for k, v in inputs.items()}
    C = a["L0_attn_x"].shape[-1]
    E, _, F = a["L0_ffn_W1"].shape
    HD = 64
    HEADS = a["L0_attn_w_q"].shape[1] // HD
    up = a["L0_attn_w_kv_up"]
    cut = HEADS * HD
    laid = {
        "x": a["L0_attn_x"],
        "w_down": a["L0_attn_w_kv_down"],
        "wq_t": a["L0_attn_w_q"].T.reshape(HEADS, HD, C).transpose(1, 0, 2),
        "wuk_t": up[:, :cut].T.reshape(HEADS, HD, C).transpose(1, 0, 2),
        "wuv_t": up[:, cut:].T.reshape(HEADS, HD, C).transpose(1, 0, 2),
        "w_out": a["L0_attn_w_out"].reshape(HEADS, HD, C).transpose(1, 0, 2),
        "centroids": a["L0_ffn_centroids"],
        "wp_t": a["L0_ffn_Wp"].T,
        "wp": a["L0_ffn_Wp"],
        "bp": a["L0_ffn_bp"].reshape(C, 1),
        "w1": a["L0_ffn_W1"].transpose(1, 0, 2),
        "b1": a["L0_ffn_b1"].reshape(E, F // 128, 128).transpose(2, 0, 1),
        "w2": a["L0_ffn_W2"].reshape(E, F // 128, 128, C).transpose(2, 0, 1, 3).reshape(128, E, F // 128 * C),
        "b2": a["L0_ffn_b2"].T,
    }
    nc = _bacc.Bacc("TRN2", target_bir_lowering=False, num_devices=1)
    arrays, args = {}, []
    for name, v in laid.items():
        v = _np.ascontiguousarray(v)
        arrays[f"in_{name}"] = v
        args.append(nc.dram_tensor(f"in_{name}", v.shape, _mybir.dt.from_np(v.dtype), kind="ExternalInput").ap())
    out = nc.dram_tensor("out", _OUT, _mybir.dt.float32, kind="ExternalOutput").ap()
    macaron_block(nc, *args, out)
    r = _run(nc, [arrays], core_ids=[0])
    return r.results[0]["out"]
```
